# Optimizing a Trainium2 kernel written in Bass

```python
import numpy as np
import jax
import jax.numpy as jnp

def _softmax(x, axis=-1):
    return jax.nn.softmax(x, axis=axis)

def _gelu(x):
    return jax.nn.gelu(x, approximate=True)

def _silu(x):
    return jax.nn.silu(x)

def _sigmoid(x):
    return jax.nn.sigmoid(x)

def _layernorm(x, axis=-1, eps=1e-05):
    m = jnp.mean(x, axis=axis, keepdims=True)
    v = jnp.var(x, axis=axis, keepdims=True)
    return (x - m) / jnp.sqrt(v + eps)

def _scatter_add(tgt, idx, src, axis=0):
    return tgt.at[idx].add(src)

def _segment_sum(src, seg, n):
    return jax.ops.segment_sum(src, seg, n)
kernel_name = 'mk_perceiver_d1_seqx_r8_b615aa'

def setup_inputs(seed: int=0):
    np.random.seed(seed)
    _w = jnp.asarray

    def _rec_inputs():
        import jax
        import jax.numpy as jnp
        _rk = jax.random.key(seed)
        x = -0.0002928 + 1 * jax.random.normal(jax.random.fold_in(_rk, 1), (32, 32, 128), jnp.float32)
        _lenS = 32 - jax.random.randint(jax.random.fold_in(_rk, 7), (32,), 0, max(1, 32 // 4) + 1, jnp.int32)
        _lenS2 = 257 - jax.random.randint(jax.random.fold_in(_rk, 8), (32,), 0, max(1, 257 // 4) + 1, jnp.int32)
        _ctx_1024P = jax.random.normal(jax.random.fold_in(_rk, 11), (32, 16, 128), jnp.float32)
        _ctx_1024c = jax.random.dirichlet(jax.random.fold_in(_rk, 511), 0.3 * jnp.ones((16,), jnp.float32), (32, 257))
        _ctx_1024t = jnp.einsum('bsk,bkd->bsd', _ctx_1024c, _ctx_1024P)
        _ctx_1024t = _ctx_1024t * jax.lax.rsqrt(jnp.mean(jnp.square(_ctx_1024t)) + 1e-12) * 0.953939
        ctx_1024 = 4.13588e-05 + 0.999923 * (_ctx_1024t + 0.3 * jax.random.normal(jax.random.fold_in(_rk, 611), (32, 257, 128), jnp.float32))
        return (x, ctx_1024)
    x, ctx_1024 = _rec_inputs()

    def _L0_xattn_setup():
        import jax, jax.numpy as jnp
        import numpy as np
        FEATURE_DIM = 128
        NUM_HEADS = 16
        HEAD_DIM = FEATURE_DIM // NUM_HEADS
        key = jax.random.key(seed)
        ks = jax.random.split(key, 11)
        B, SQ, SKV, D = (4, 128, 256, FEATURE_DIM)
        s = 1.0 / np.sqrt(D)
        return {'query': jax.random.normal(ks[0], (B, SQ, D), jnp.float32), 'key': jax.random.normal(ks[1], (B, SKV, D), jnp.float32), 'value': jax.random.normal(ks[2], (B, SKV, D), jnp.float32), 'wq': jax.random.normal(ks[3], (D, D), jnp.float32) * s, 'bq': jnp.zeros((D,), jnp.float32), 'wk': jax.random.normal(ks[4], (D, D), jnp.float32) * s, 'bk': jnp.zeros((D,), jnp.float32), 'wv': jax.random.normal(ks[5], (D, D), jnp.float32) * s, 'bv': jnp.zeros((D,), jnp.float32), 'wo': jax.random.normal(ks[6], (D, D), jnp.float32) * s, 'bo': jnp.zeros((D,), jnp.float32)}
    _L0_xattn_all = _L0_xattn_setup()
    _L0_xattn_in = {k: v for k, v in _L0_xattn_all.items() if k in ('wq', 'bq', 'wk', 'bk', 'wv', 'bv', 'wo', 'bo')}
    del _L0_xattn_all

    def _L0_attn_setup():
        import jax, jax.numpy as jnp
        import numpy as np
        B_, T_, D_ = (8, 512, 128)

        def _reference_tuple_inner(u, WA, WB, WAf, WBf, w1, w2, b, Wc):
            bsz, seq_len, _ = u.shape
            xf = jnp.concatenate([u[:, :1], jnp.einsum('btd,ed->bte', u[:, 1:], WB)], axis=1)
            xb = jnp.concatenate([jnp.einsum('btd,ed->bte', u[:, 1:], WBf), u[:, -1:]], axis=1)
            gamma = jax.nn.sigmoid(xf @ w1.T + xb @ w2.T + b)
            y = gamma * (xf + xb) + (1.0 - gamma) * u
            final_output = jax.nn.sigmoid(y @ Wc.T).reshape(bsz, seq_len)
            return (y, gamma, final_output)
        key = jax.random.key(seed)
        ks = jax.random.split(key, 9)
        s = 1.0 / np.sqrt(D_)
        return {'u': jax.random.normal(ks[0], (B_, T_, D_), dtype=jnp.float32), 'WA': jax.random.uniform(ks[1], (D_, D_), jnp.float32, -s, s), 'WB': jax.random.uniform(ks[2], (D_, D_), jnp.float32, -s, s), 'WAf': jax.random.uniform(ks[3], (D_, D_), jnp.float32, -s, s), 'WBf': jax.random.uniform(ks[4], (D_, D_), jnp.float32, -s, s), 'w1': jax.random.uniform(ks[5], (1, D_), jnp.float32, -s, s), 'w2': jax.random.uniform(ks[6], (1, D_), jnp.float32, -s, s), 'b': jnp.zeros((1,), dtype=jnp.float32), 'Wc': jax.random.uniform(ks[7], (1, D_), jnp.float32, -s, s)}
    _L0_attn_all = _L0_attn_setup()
    _L0_attn_in = {k: v for k, v in _L0_attn_all.items() if k in ('WA', 'WB', 'WAf', 'WBf', 'w1', 'w2', 'b', 'Wc')}
    del _L0_attn_all

    def _L0_ffn_setup():
        import jax, jax.numpy as jnp
        import numpy as np
        E = 8
        TOPK = 2
        D = 128
        F = 512
        B, S = (2, 64)

        def _gmm(x, W, expert_onehot):
            return jnp.einsum('te,td,edf->tf', expert_onehot, x, W)
        key = jax.random.key(seed)
        k1, k2, k3, k4, k5 = jax.random.split(key, 5)
        scale_d = 1.0 / np.sqrt(D)
        scale_f = 1.0 / np.sqrt(F)
        return {'inputs': jax.random.normal(k1, (B, S, D), jnp.float32), 'gate_kernel': jax.random.normal(k2, (D, E), jnp.float32) * scale_d, 'w0': jax.random.normal(k3, (E, D, F), jnp.float32) * scale_d, 'w1': jax.random.normal(k4, (E, D, F), jnp.float32) * scale_d, 'wo': jax.random.normal(k5, (E, F, D), jnp.float32) * scale_f}
    _L0_ffn_all = _L0_ffn_setup()
    _L0_ffn_in = {k: v for k, v in _L0_ffn_all.items() if k in ('gate_kernel', 'w0', 'w1', 'wo')}
    del _L0_ffn_all
    return {'x': x, 'ctx_1024': ctx_1024, 'L0_xattn_wq': _L0_xattn_in['wq'], 'L0_xattn_bq': _L0_xattn_in['bq'], 'L0_xattn_wk': _L0_xattn_in['wk'], 'L0_xattn_bk': _L0_xattn_in['bk'], 'L0_xattn_wv': _L0_xattn_in['wv'], 'L0_xattn_bv': _L0_xattn_in['bv'], 'L0_xattn_wo': _L0_xattn_in['wo'], 'L0_xattn_bo': _L0_xattn_in['bo'], 'L0_attn_WA': _L0_attn_in['WA'], 'L0_attn_WB': _L0_attn_in['WB'], 'L0_attn_WAf': _L0_attn_in['WAf'], 'L0_attn_WBf': _L0_attn_in['WBf'], 'L0_attn_w1': _L0_attn_in['w1'], 'L0_attn_w2': _L0_attn_in['w2'], 'L0_attn_b': _L0_attn_in['b'], 'L0_attn_Wc': _L0_attn_in['Wc'], 'L0_ffn_gate_kernel': _L0_ffn_in['gate_kernel'], 'L0_ffn_w0': _L0_ffn_in['w0'], 'L0_ffn_w1': _L0_ffn_in['w1'], 'L0_ffn_wo': _L0_ffn_in['wo']}

def reference(x, ctx_1024, L0_xattn_wq, L0_xattn_bq, L0_xattn_wk, L0_xattn_bk, L0_xattn_wv, L0_xattn_bv, L0_xattn_wo, L0_xattn_bo, L0_attn_WA, L0_attn_WB, L0_attn_WAf, L0_attn_WBf, L0_attn_w1, L0_attn_w2, L0_attn_b, L0_attn_Wc, L0_ffn_gate_kernel, L0_ffn_w0, L0_ffn_w1, L0_ffn_wo):
    import jax
    import jax.numpy as jnp

    def _L0_xattn_ref(query, key, value, wq, bq, wk, bk, wv, bv, wo, bo):
        import jax, jax.numpy as jnp
        import numpy as np
        FEATURE_DIM = 128
        NUM_HEADS = 16
        HEAD_DIM = FEATURE_DIM // NUM_HEADS
        B, SQ, D = query.shape
        H, HD = (NUM_HEADS, HEAD_DIM)
        q = (query @ wq.T + bq).reshape(B, SQ, H, HD).transpose(0, 2, 1, 3)
        k = (key @ wk.T + bk).reshape(B, -1, H, HD).transpose(0, 2, 1, 3)
        v = (value @ wv.T + bv).reshape(B, -1, H, HD).transpose(0, 2, 1, 3)
        scores = jnp.einsum('bhqd,bhkd->bhqk', q, k) / jnp.sqrt(jnp.asarray(HD, q.dtype))
        attn = jax.nn.softmax(scores, axis=-1)
        ctx = jnp.einsum('bhqk,bhkd->bhqd', attn, v)
        ctx = ctx.transpose(0, 2, 1, 3).reshape(B, SQ, D)
        return ctx @ wo.T + bo

    def _L0_attn_ref(u, WA, WB, WAf, WBf, w1, w2, b, Wc):
        import jax, jax.numpy as jnp
        import numpy as np
        B_, T_, D_ = (8, 512, 128)

        def _reference_tuple_inner(u, WA, WB, WAf, WBf, w1, w2, b, Wc):
            bsz, seq_len, _ = u.shape
            xf = jnp.concatenate([u[:, :1], jnp.einsum('btd,ed->bte', u[:, 1:], WB)], axis=1)
            xb = jnp.concatenate([jnp.einsum('btd,ed->bte', u[:, 1:], WBf), u[:, -1:]], axis=1)
            gamma = jax.nn.sigmoid(xf @ w1.T + xb @ w2.T + b)
            y = gamma * (xf + xb) + (1.0 - gamma) * u
            final_output = jax.nn.sigmoid(y @ Wc.T).reshape(bsz, seq_len)
            return (y, gamma, final_output)
        return _reference_tuple_inner(u, WA, WB, WAf, WBf, w1, w2, b, Wc)[0]

    def _L0_ffn_ref(inputs, gate_kernel, w0, w1, wo):
        import jax, jax.numpy as jnp
        import numpy as np
        E = 8
        TOPK = 2
        D = 128
        F = 512
        B, S = (2, 64)

        def _gmm(x, W, expert_onehot):
            return jnp.einsum('te,td,edf->tf', expert_onehot, x, W)
        dtype = inputs.dtype
        gate_logits = jnp.einsum('bsd,de->bse', inputs, gate_kernel)
        weights, selected_experts = jax.lax.top_k(gate_logits, TOPK)
        weights = jax.nn.softmax(weights.astype(jnp.float32), axis=-1).astype(dtype)
        inputs_2d = jnp.reshape(inputs, (-1, D))
        flat_sel = jnp.ravel(selected_experts)
        sort_idx = jnp.argsort(flat_sel)
        rep = jnp.repeat(inputs_2d, TOPK, axis=0)
        sorted_hidden = jnp.take(rep, sort_idx, axis=0)
        T = flat_sel.shape[0]
        group_sizes = jnp.zeros((E,), jnp.int32).at[flat_sel].add(1)
        expert_ids = jnp.repeat(jnp.arange(E), group_sizes, total_repeat_length=T)
        onehot = jax.nn.one_hot(expert_ids, E, dtype=dtype)
        layer_1 = _gmm(sorted_hidden, w0, onehot)
        layer_2 = _gmm(sorted_hidden, w1, onehot)
        intermediate = jax.nn.silu(layer_1) * layer_2
        layer_3 = _gmm(intermediate, wo, onehot)
        unsort = jnp.take(layer_3, jnp.argsort(sort_idx), axis=0)
        combined = unsort * jnp.ravel(weights)[:, None]
        out = jnp.sum(combined.reshape(-1, TOPK, D), axis=1)
        return out.reshape(inputs.shape).astype(dtype)
    x = x + _L0_xattn_ref(_layernorm(x, axis=-1), ctx_1024, ctx_1024, L0_xattn_wq, L0_xattn_bq, L0_xattn_wk, L0_xattn_bk, L0_xattn_wv, L0_xattn_bv, L0_xattn_wo, L0_xattn_bo)
    x = x + _L0_attn_ref(_layernorm(x, axis=-1), L0_attn_WA, L0_attn_WB, L0_attn_WAf, L0_attn_WBf, L0_attn_w1, L0_attn_w2, L0_attn_b, L0_attn_Wc)
    x = x + _L0_ffn_ref(_layernorm(x, axis=-1), L0_ffn_gate_kernel, L0_ffn_w0, L0_ffn_w1, L0_ffn_wo)
    return x

_drawn_inputs = setup_inputs


def setup_inputs(seed=0):
    import zlib

    import numpy as np

    out = dict(_drawn_inputs(seed))
    spreads = {'L0_xattn_bq': (0.0, 0.1),
     'L0_xattn_bk': (0.0, 0.1),
     'L0_xattn_bv': (0.0, 0.1),
     'L0_xattn_bo': (0.0, 0.1)}
    factors = {}
    for name, (base, spread) in spreads.items():
        noise = np.random.default_rng([zlib.crc32(name.encode()), seed]).standard_normal(out[name].shape)
        drawn = base * np.exp(spread * noise) if base else spread * noise
        out[name] = jnp.asarray(drawn.astype(out[name].dtype))
    for name, factor in factors.items():
        out[name] = (out[name] * factor).astype(out[name].dtype)
    return out
```

```python
from contextlib import ExitStack

import concourse.bass as bass
from concourse import mybir

F32 = mybir.dt.float32
U32 = mybir.dt.uint32
ALU = mybir.AluOpType
ACT = mybir.ActivationFunctionType
AX = mybir.AxisListType

B, SQ, D = 32, 32, 128
SKV = 257
KEYS = 256
H, HD = 16, 8
G, J = 4, 4
TOK = B * SQ
NT = TOK // 128
BPT = 128 // SQ
E, F, FC = 8, 512, 4
HALF = TOK // 2
EPS = 1e-5
Q_SCALE = float(HD) ** -0.5

W_Q, W_K, W_V, W_O, W_B, W_BF = (slice(n * D, (n + 1) * D) for n in range(6))
V_BQ, V_BK, V_W1, V_W2, V_B = (slice(n, n + 1) for n in range(5))


def build(nc, x, ctx_keys, ctx_last, weights, vectors, rows, gate, w01, wo, out):
    with ExitStack() as stack:
        def sb(name, shape, dt=F32):
            return stack.enter_context(nc.sbuf_tensor(name, shape, dt))

        def sem(name):
            return stack.enter_context(nc.semaphore(name))

        x_tok = sb("x_tok", [128, NT, D])
        x1_tok = sb("x1_tok", [128, NT, D])
        x2_tok = sb("x2_tok", [128, NT, D])
        w_sb = sb("w_sb", [128, 6 * D])
        vec_sb = sb("vec_sb", [128, 5])
        row_sb = sb("row_sb", [128, 2, D])
        gate_sb = sb("gate_sb", [128, E])
        last_sb = sb("last_sb", [128, B])
        last_rep = sb("last_rep", [128, B, SQ])
        ident = sb("ident", [128, 128])
        head_mask = sb("head_mask", [128, H])
        expert_no = sb("expert_no", [128, E])
        norm_tok = sb("norm_tok", [128, NT, D])
        norm_ft = sb("norm_ft", [128, TOK])
        stats = sb("stats", [128, NT, 6])
        mean_var = sb("mean_var", [128, NT, 2])
        var_eps = sb("var_eps", [128, NT])
        minus_half = sb("minus_half", [128, NT])
        rstd = sb("rstd", [128, NT])
        q_ft = sb("q_ft", [128, TOK])
        k_last = sb("k_last", [128, B])
        v_last = sb("v_last", [128, NT, D])
        ctx_sb = [sb(f"ctx_sb{n}", [128, KEYS]) for n in range(BPT)]
        k_sb = [sb(f"k_sb{n}", [128, SKV]) for n in range(2)]
        v_sb = [sb(f"v_sb{n}", [128, 2, D]) for n in range(2)]
        qbd_sb = [sb(f"qbd_sb{n}", [128, H, SQ]) for n in range(2)]
        neg_max = [sb(f"neg_max{n}", [128, G]) for n in range(2)]
        p_sb = [sb(f"p_sb{n}", [128, G, SKV]) for n in range(2)]
        pt_sb = [sb(f"pt_sb{n}", [128, 2, G * 128]) for n in range(2)]
        sum_last = sb("sum_last", [128, 2, B, G])
        sum_last_tok = sb("sum_last_tok", [128, 2, NT, H])
        r_sum = sb("r_sum", [128, NT, H])
        att_tok = sb("att_tok", [128, NT, D])
        att_ft = sb("att_ft", [128, TOK])
        xf_ft = sb("xf_ft", [128, B, SQ])
        xb_ft = sb("xb_ft", [128, B, SQ])
        s_ft = sb("s_ft", [128, TOK])
        gamma = sb("gamma", [128, NT])
        logits = sb("logits", [128, NT, E])
        top = sb("top", [128, NT, 8])
        top_at = sb("top_at", [128, NT, 8], U32)
        top_no = sb("top_no", [128, NT, 2])
        top_d = sb("top_d", [128, NT])
        top_w = sb("top_w", [128, NT, 2])
        pick = sb("pick", [128, 2, NT, E])
        share = sb("share", [128, NT, E])
        w01_sb = [sb(f"w01_sb{n}", [128, 2, F]) for n in range(2)]
        wo_sb = [sb(f"wo_sb{n}", [128, FC, D]) for n in range(2)]
        silu_sb = [sb(f"silu_sb{n}", [128, HALF]) for n in range(2)]
        hid_sb = [sb(f"hid_sb{n}", [128, FC, HALF]) for n in range(2)]

        bank = [stack.enter_context(nc.psum_tensor(f"bank{n}", [128, 512], F32)) for n in range(8)]
        s_bank = bank[0:4]
        pt_bank = bank[4:6]
        kv_bank = bank[6]
        o_bank = bank[7]

        x_in, w_in, vec_in, row_in, gate_in, last_in = (
            sem(n) for n in ("x_in", "w_in", "vec_in", "row_in", "gate_in", "last_in"))
        ctx_in = [sem(f"ctx_in{n}") for n in range(BPT)]
        expert_in = [sem(f"expert_in{n}") for n in range(2)]
        out_done = sem("out_done")
        kv_done, k_ready, k_last_ready, v_ready, qbd_ready = (
            sem(n) for n in ("kv_done", "k_ready", "k_last_ready", "v_ready", "qbd_ready"))
        scores_done, max_ready, probs_ready, pt_done, pt0_ready, pt1_ready = (
            sem(n) for n in ("scores_done", "max_ready", "probs_ready", "pt_done", "pt0_ready", "pt1_ready"))
        last_kept, pv_done, o_taken = (sem(n) for n in ("last_kept", "pv_done", "o_taken"))
        hid_done, silu_ready, hid_ready, y_done, y_added = (
            sem(n) for n in ("hid_done", "silu_ready", "hid_ready", "y_done", "y_added"))
        pool_step, dve_step, act_step = sem("pool_step"), sem("dve_step"), sem("act_step")
        consts_ready, last_rep_ready, xbo_ready = (
            sem(n) for n in ("consts_ready", "last_rep_ready", "xbo_ready"))
        var_ready, rstd_ready, normed, norm_turned, norm_ft_ready = (
            sem(n) for n in ("var_ready", "rstd_ready", "normed", "norm_turned", "norm_ft_ready"))
        pre_done, q_ready, v_last_ready, kl_ready = (
            sem(n) for n in ("pre_done", "q_ready", "v_last_ready", "kl_ready"))
        att_ready, att_turned, att_ft_ready, wo_done = (
            sem(n) for n in ("att_ready", "att_turned", "att_ft_ready", "wo_done"))
        mix_done, xf_ready, edges_ready, s_ready, mix2_done, gamma_ready = (
            sem(n) for n in ("mix_done", "xf_ready", "edges_ready", "s_ready", "mix2_done", "gamma_ready"))
        logits_done, top_ready, top_w_ready, share_ready = (
            sem(n) for n in ("logits_done", "top_ready", "top_w_ready", "share_ready"))

        block = stack.enter_context(nc.Block())

        def tile(t):
            return slice(t * 128, (t + 1) * 128)

        @block.sync
        def _(sp):
            sp.dma_start(x_tok[:], x.rearrange("(t p) d -> p t d", p=128)).then_inc(x_in, 16)
            sp.dma_start(w_sb[:], weights).then_inc(w_in, 16)
            sp.dma_start(vec_sb[:], vectors).then_inc(vec_in, 16)
            sp.dma_start(last_sb[:], ctx_last).then_inc(last_in, 16)
            for k in range(BPT):
                sp.dma_start(ctx_sb[k][:], ctx_keys[:, k, :]).then_inc(ctx_in[k], 16)
            sp.dma_start(row_sb[:], rows.partition_broadcast(128)).then_inc(row_in, 16)
            sp.dma_start(gate_sb[:], gate).then_inc(gate_in, 16)
            for n in range(2):
                sp.dma_start(w01_sb[n][:], w01[n]).then_inc(expert_in[n], 16)
                sp.dma_start(wo_sb[n][:], wo[n]).then_inc(expert_in[n], 16)
            with sp.Fori(1, B // BPT) as i:
                for k in range(BPT):
                    sp.wait_ge(kv_done, BPT * i + (k - BPT + 1))
                    sp.dma_start(ctx_sb[k][:], ctx_keys[:, BPT * i + k, :]).then_inc(ctx_in[k], 16)
            with sp.Fori(1, E // 2) as i:
                for n in range(2):
                    sp.wait_ge(hid_done, 16 * i + 8 * (n - 1))
                    sp.dma_start(w01_sb[n][:], w01[2 * i + n]).then_inc(expert_in[n], 16)
                    sp.wait_ge(y_done, 4 * i + 2 * (n - 1))
                    sp.dma_start(wo_sb[n][:], wo[2 * i + n]).then_inc(expert_in[n], 16)
            for half in range(2):
                sp.wait_ge(y_added, 2 * E - 1 + half)
                sp.dma_start(out.rearrange("(t p) d -> p t d", p=128)[:, 4 * half:4 * half + 4, :],
                             x2_tok[:, 4 * half:4 * half + 4, :]).then_inc(out_done, 16)
            sp.wait_ge(out_done, 32)

        @block.gpsimd
        def _(pool):
            steps = [0]

            def own(ins):
                steps[0] += 1
                ins.then_inc(pool_step, 1)
                pool.wait_ge(pool_step, steps[0])

            def inverse_root(nth):
                pool.wait_ge(var_ready, nth)
                pool.tensor_tensor(rstd[:], var_eps[:], minus_half[:], ALU.pow).then_inc(rstd_ready, 1)

            own(pool.memset(minus_half[:], -0.5))
            inverse_root(1)
            own(pool.memset(ident[:], 0.0))
            pool.affine_select(out=ident[:], in_=ident[:], compare_op=ALU.not_equal, fill=1.0, base=0,
                               pattern=[[-1, 128]], channel_multiplier=1).then_inc(consts_ready, 1)
            own(pool.memset(head_mask[:], 1.0))
            own(pool.affine_select(out=head_mask[:], in_=head_mask[:], compare_op=ALU.is_ge, fill=0.0,
                                   base=0, pattern=[[-HD, H]], channel_multiplier=1))
            own(pool.affine_select(out=head_mask[:], in_=head_mask[:], compare_op=ALU.is_ge, fill=0.0,
                                   base=HD - 1, pattern=[[HD, H]], channel_multiplier=-1))
            pool.wait_ge(last_in, 16)
            pool.tensor_copy(last_rep[:], last_sb[:].unsqueeze(2).to_broadcast([128, B, SQ])
                             ).then_inc(last_rep_ready, 1)
            pool.iota(expert_no[:], [[1, E]], base=0, channel_multiplier=0,
                      allow_small_or_imprecise_dtypes=True).then_inc(consts_ready, 1)
            pool.wait_ge(q_ready, 1)
            pool.wait_ge(kl_ready, 1)

            def batch(i, k, first=False):
                p = k % 2
                if not (first and k < 2):
                    pool.wait_ge(scores_done, G * BPT * i + G * (k - 1))
                pool.tensor_copy(k_sb[p][:, KEYS:SKV], k_last[:, bass.ds(BPT * i + k, 1)]
                                 ).then_inc(k_last_ready, 1)
                q = q_ft[:, bass.ds(SQ * BPT * i + SQ * k, SQ)].unsqueeze(1).to_broadcast([128, H, SQ])
                m = head_mask[:].unsqueeze(2).to_broadcast([128, H, SQ])
                pool.tensor_tensor(qbd_sb[p][:], q, m, ALU.mult).then_inc(qbd_ready, 1)

            def keep_last(i, k):
                pool.wait_ge(probs_ready, G * BPT * i + G * (k + 1))
                pool.tensor_copy(sum_last[:, 1, bass.ds(BPT * i + k, 1), :].rearrange("p a g -> p (a g)"),
                                 p_sb[k % 2][:, :, KEYS]).then_inc(last_kept, 1)

            batch(0, 0, True)
            batch(0, 1, True)
            for k in range(2, BPT):
                batch(0, k, True)
                keep_last(0, k - 2)
            with pool.Fori(1, B // BPT) as i:
                for k in range(BPT):
                    batch(i, k)
                    if k < 2:
                        keep_last(i - 1, k + 2)
                    else:
                        keep_last(i, k - 2)
            keep_last(B // BPT - 1, 2)
            keep_last(B // BPT - 1, 3)

            pool.wait_ge(row_in, 16)
            pool.wait_ge(x_in, 16)
            pool.tensor_tensor(x1_tok[:], x_tok[:], row_sb[:, 1, :].unsqueeze(1).to_broadcast([128, NT, D]),
                               ALU.add).then_inc(xbo_ready, 1)
            inverse_root(2)
            u = norm_ft[:].rearrange("p (b q) -> p b q", q=SQ)
            pool.wait_ge(norm_ft_ready, 4)
            pool.tensor_copy(xf_ft[:, :, 0:1], u[:, :, 0:1]).then_inc(edges_ready, 1)
            pool.tensor_copy(xb_ft[:, :, SQ - 1:SQ], u[:, :, SQ - 1:SQ]).then_inc(edges_ready, 1)
            inverse_root(3)

        @block.scalar
        def _(act):
            act.wait_ge(vec_in, 16)
            act.wait_ge(pre_done, 2)
            act.activation(k_last[:], kv_bank[:, 0:B], ACT.Identity, bias=vec_sb[:, V_BK]).then_inc(kl_ready, 1)
            for n in range(2):
                act.activation(v_last[:, 4 * n:4 * n + 4, :].rearrange("p t d -> p (t d)"), bank[2 + n][:],
                               ACT.Copy).then_inc(v_last_ready, 1)

            def keys_values(i, k, first=False):
                act.wait_ge(kv_done, BPT * i + (k + 1))
                if not (first and k < 2):
                    act.wait_ge(scores_done, G * BPT * i + G * (k - 1))
                act.activation(k_sb[k % 2][:, 0:KEYS], kv_bank[:, 0:KEYS], ACT.Identity,
                               bias=vec_sb[:, V_BK]).then_inc(k_ready, 1)
                if not (first and k < 2):
                    act.wait_ge(pv_done, BPT * i + (k - 1))
                act.activation(v_sb[k % 2][:].rearrange("p t d -> p (t d)"), kv_bank[:, KEYS:512],
                               ACT.Copy).then_inc(v_ready, 1)

            def softmax(i, k, first=False):
                p = k % 2
                if not (first and k < 2):
                    act.wait_ge(pt_done, 2 * BPT * i + 2 * (k - 1))
                    act.wait_ge(last_kept, BPT * i + (k - 1))
                for g in range(G):
                    act.wait_ge(max_ready, G * BPT * i + (G * k + g + 1))
                    act.activation(p_sb[p][:, g, :], s_bank[g][:, 0:SKV], ACT.Exp, bias=neg_max[p][:, g:g + 1],
                                   accum_out=sum_last[:, 0, bass.ds(BPT * i + k, 1), g]
                                   ).then_inc(probs_ready, 1)

            def turned(i, k, first=False):
                act.wait_ge(pt_done, 2 * BPT * i + 2 * (k + 1))
                if not (first and k < 2):
                    act.wait_ge(pv_done, BPT * i + (k - 1))
                act.activation(pt_sb[k % 2][:, 1, :], pt_bank[1][:], ACT.Copy).then_inc(pt1_ready, 1)

            def group(i, first=False, last=False):
                for k in range(BPT):
                    if first and k == 0:
                        keys_values(i, 0, True)
                    softmax(i, k, first)
                    if not (last and k == BPT - 1):
                        keys_values(i if k < BPT - 1 else i + 1, (k + 1) % BPT, first and k < BPT - 1)
                    turned(i, k, first)

            group(0, first=True)
            with act.Fori(1, B // BPT - 1) as i:
                group(i)
            group(B // BPT - 1, last=True)

            for n in range(2):
                act.wait_ge(att_turned, n + 1)
                act.activation(att_ft[:, n * HALF:(n + 1) * HALF], bank[4 + n][:], ACT.Copy).then_inc(att_ft_ready, 1)
            act.wait_ge(norm_turned, 4)
            act.activation(norm_ft[:, HALF:TOK], bank[5][:], ACT.Copy).then_inc(norm_ft_ready, 1)
            for n in range(2):
                act.wait_ge(mix_done, n + 1)
                act.activation(xf_ft[:, 16 * n:16 * n + 16, 1:SQ],
                               bank[n][:].rearrange("p (b q) -> p b q", q=SQ)[:, :, 1:SQ],
                               ACT.Copy).then_inc(xf_ready, 1)
            act.wait_ge(mix2_done, 1)
            act.activation(gamma[:], bank[6][:, 0:NT], ACT.Sigmoid, bias=vec_sb[:, V_B]).then_inc(gamma_ready, 1)
            act.wait_ge(norm_turned, 6)
            act.activation(norm_ft[:, HALF:TOK], bank[5][:], ACT.Copy).then_inc(norm_ft_ready, 1)
            act.wait_ge(top_ready, 1)
            act.activation(top_w[:, :, 0], top_d[:], ACT.Sigmoid).then_inc(top_w_ready, 1)
            act.activation(top_w[:, :, 1], top_d[:], ACT.Sigmoid, scale=-1.0).then_inc(top_w_ready, 1)

            def silus(i, first=False):
                for n in range(2 * 2 * FC):
                    act.wait_ge(hid_done, 16 * i + (n + 1))
                    if not (first and n < 2):
                        act.wait_ge(hid_ready, 16 * i + (n - 1))
                    act.activation(silu_sb[n % 2][:], bank[n % 2][:], ACT.Silu).then_inc(silu_ready, 1)

            silus(0, True)
            with act.Fori(1, E // 2) as i:
                silus(i)

        @block.tensor
        def _(pe):
            def turn(src, dst_banks, count_sem):
                for n in range(2):
                    for t in range(4):
                        last = pe.transpose(dst_banks[n][:, tile(t)], src[:, 4 * n + t, :], ident[:])
                    last.then_inc(count_sem, 1)

            pe.wait_ge(last_in, 16)
            pe.wait_ge(w_in, 16)
            pe.wait_ge(last_rep_ready, 1)
            pe.matmul(kv_bank[:, 0:B], w_sb[:, W_K], last_sb[:], start=True, stop=True)
            for t in range(NT):
                last = pe.matmul(bank[2 + t // 4][:, tile(t % 4)],
                                 last_rep[:, BPT * t:BPT * (t + 1), :].rearrange("p b q -> p (b q)"),
                                 w_sb[:, W_V], start=True, stop=True)
            last.then_inc(pre_done, 2)
            pe.wait_ge(consts_ready, 1)
            pe.wait_ge(normed, 1)
            turn(norm_tok, bank[4:6], norm_turned)
            for n in range(2):
                pe.wait_ge(norm_ft_ready, n + 1)
                pe.matmul(bank[n][:], w_sb[:, W_Q], norm_ft[:, n * HALF:(n + 1) * HALF],
                          start=True, stop=True).then_inc(pre_done, 1)

            def keys_values(i, k, first=False):
                if first and k == 0:
                    pe.wait_ge(kl_ready, 1)
                else:
                    pe.wait_ge(k_ready, BPT * i + k)
                    pe.wait_ge(v_ready, BPT * i + k)
                pe.wait_ge(ctx_in[k], 16 * i + 16)
                pe.matmul(kv_bank[:, 0:KEYS], w_sb[:, W_K], ctx_sb[k][:], start=True, stop=True)
                for t in range(2):
                    last = pe.matmul(kv_bank[:, KEYS + 128 * t:KEYS + 128 * (t + 1)], ctx_sb[k][:, tile(t)],
                                     w_sb[:, W_V], start=True, stop=True)
                last.then_inc(kv_done, 1)

            def scores(i, k, first=False):
                pe.wait_ge(k_ready, BPT * i + (k + 1))
                pe.wait_ge(k_last_ready, BPT * i + (k + 1))
                pe.wait_ge(qbd_ready, BPT * i + (k + 1))
                for g in range(G):
                    if first and k == 0:
                        if g == 0:
                            pe.wait_ge(q_ready, 1)
                            pe.wait_ge(v_last_ready, 2)
                    else:
                        pe.wait_ge(probs_ready, G * BPT * i + (G * (k - 1) + g + 1))
                    pe.matmul(s_bank[g][:, 0:SKV],
                              qbd_sb[k % 2][:, J * g:J * (g + 1), :].rearrange("p h q -> p (h q)"),
                              k_sb[k % 2][:], start=True, stop=True).then_inc(scores_done, 1)

            def turn_probs(i, k, first=False):
                pe.wait_ge(probs_ready, G * BPT * i + G * (k + 1))
                for t in range(2):
                    if not (first and k == 0):
                        pe.wait_ge((pt0_ready, pt1_ready)[t], BPT * i + k)
                    for g in range(G):
                        last = pe.transpose(pt_bank[t][:, tile(g)], p_sb[k % 2][:, g, tile(t)], ident[:])
                    last.then_inc(pt_done, 1)

            def weigh_values(i, k, first=False):
                pe.wait_ge(v_ready, BPT * i + (k + 1))
                pe.wait_ge(pt0_ready, BPT * i + (k + 1))
                pe.wait_ge(pt1_ready, BPT * i + (k + 1))
                if not (first and k == 0):
                    pe.wait_ge(o_taken, BPT * i + k)
                for g in range(G):
                    for t in range(2):
                        last = pe.matmul(o_bank[:, tile(g)], pt_sb[k % 2][:, t, tile(g)], v_sb[k % 2][:, t, :],
                                         start=(t == 0), stop=(t == 1))
                last.then_inc(pv_done, 1)

            def group(i, first=False, last=False):
                for k in range(BPT):
                    more = not (last and k == BPT - 1)
                    after = (i, k + 1) if k < BPT - 1 else (i + 1, 0)
                    turn_probs(i, k, first)
                    if more:
                        scores(*after)
                    weigh_values(i, k, first)
                    if more and not (last and k == BPT - 2):
                        keys_values(*((i, k + 2) if k < BPT - 2 else (i + 1, k - 2)))

            keys_values(0, 0, True)
            scores(0, 0, True)
            keys_values(0, 1)
            group(0, first=True)
            with pe.Fori(1, B // BPT - 1) as i:
                group(i)
            group(B // BPT - 1, last=True)

            pe.wait_ge(att_ready, 1)
            turn(att_tok, bank[4:6], att_turned)
            for t in range(NT):
                if t % 4 == 0:
                    pe.wait_ge(att_ft_ready, t // 4 + 1)
                last = pe.matmul(bank[t // 4][:, tile(t % 4)], att_ft[:, tile(t)], w_sb[:, W_O],
                                 start=True, stop=True)
            last.then_inc(wo_done, 1)
            pe.wait_ge(normed, 2)
            turn(norm_tok, bank[4:6], norm_turned)
            pe.wait_ge(norm_ft_ready, 4)
            for m in range(2):
                for n in range(2):
                    pe.matmul(bank[2 * m + n][:], w_sb[:, (W_B, W_BF)[m]], norm_ft[:, n * HALF:(n + 1) * HALF],
                              start=True, stop=True).then_inc(mix_done, 1)
            pe.wait_ge(xf_ready, 2)
            pe.wait_ge(s_ready, 1)
            for t in range(NT):
                for m, part in enumerate((xf_ft, xb_ft)):
                    last = pe.matmul(bank[6][:, t:t + 1],
                                     part[:, BPT * t:BPT * (t + 1), :].rearrange("p b q -> p (b q)"),
                                     vec_sb[:, (V_W1, V_W2)[m]], start=(m == 0), stop=(m == 1))
            last.then_inc(mix2_done, 1)
            for n in range(2):
                for t in range(4):
                    last = pe.transpose(bank[4 + n][:, tile(t)], s_ft[:, tile(4 * n + t)], ident[:])
            last.then_inc(mix2_done, 1)
            pe.wait_ge(normed, 3)
            turn(norm_tok, bank[4:6], norm_turned)
            pe.wait_ge(norm_ft_ready, 6)
            pe.wait_ge(gate_in, 16)
            for t in range(NT):
                last = pe.matmul(bank[7][:, E * t:E * (t + 1)], norm_ft[:, tile(t)], gate_sb[:],
                                 start=True, stop=True)
            last.then_inc(logits_done, 1)

            def hidden(i, n, h, first=False):
                if h == 0:
                    pe.wait_ge(expert_in[n], 32 * i + 32)
                for c in range(FC):
                    at = 2 * FC * n + FC * h + c
                    if not (first and at < 2):
                        pe.wait_ge(hid_ready, 16 * i + (at - 1))
                    for m in range(2):
                        last = pe.matmul(bank[2 * m + at % 2][:], w01_sb[n][:, m, tile(c)],
                                         norm_ft[:, h * HALF:(h + 1) * HALF], start=True, stop=True)
                    last.then_inc(hid_done, 1)

            def expert_out(i, n, h, first=False):
                at = 2 * n + h
                pe.wait_ge(hid_ready, 16 * i + 4 * (at + 1))
                if first and at < 2:
                    pe.wait_ge(top_ready, 1)
                else:
                    pe.wait_ge(y_added, 4 * i + (at - 1))
                for t in range(4):
                    for c in range(FC):
                        last = pe.matmul(bank[6 + h][:, tile(t)], hid_sb[h][:, c, tile(t)], wo_sb[n][:, c, :],
                                         start=(c == 0), stop=(c == FC - 1))
                last.then_inc(y_done, 1)

            def two_experts(i, first=False):
                hidden(i, 0, 0, first)
                if not first:
                    expert_out(i - 1, 1, 1)
                hidden(i, 0, 1)
                expert_out(i, 0, 0, first)
                hidden(i, 1, 0)
                expert_out(i, 0, 1, first)
                hidden(i, 1, 1)
                expert_out(i, 1, 0)

            two_experts(0, True)
            with pe.Fori(1, E // 2) as i:
                two_experts(i)
            expert_out(E // 2 - 1, 1, 1)

        @block.vector
        def _(dve):
            steps = [0]

            def own(ins):
                steps[0] += 1
                ins.then_inc(dve_step, 1)
                dve.wait_ge(dve_step, steps[0])

            def layer_norm(src, nth):
                for t in range(NT):
                    last = dve.bn_stats(stats[:, t, :], src[:, t, :])
                own(last)
                for t in range(NT):
                    last = dve.bn_aggr(mean_var[:, t, :], stats[:, t, :])
                own(last)
                dve.tensor_scalar(var_eps[:], mean_var[:, :, 1], EPS, None, ALU.add).then_inc(var_ready, 1)
                dve.wait_ge(rstd_ready, nth)
                for t in range(NT):
                    last = dve.tensor_scalar(norm_tok[:, t, :], src[:, t, :], mean_var[:, t, 0:1],
                                             rstd[:, t:t + 1], ALU.subtract, ALU.mult)
                last.then_inc(normed, 1)

            dve.wait_ge(x_in, 16)
            layer_norm(x_tok, 1)
            for n in range(2):
                dve.wait_ge(norm_turned, n + 1)
                dve.tensor_copy(norm_ft[:, n * HALF:(n + 1) * HALF], bank[4 + n][:]).then_inc(norm_ft_ready, 1)
            dve.wait_ge(vec_in, 16)
            for n in range(2):
                dve.wait_ge(pre_done, 3 + n)
                last = dve.tensor_scalar(q_ft[:, n * HALF:(n + 1) * HALF], bank[n][:], vec_sb[:, V_BQ], Q_SCALE,
                                         ALU.add, ALU.mult)
            last.then_inc(q_ready, 1)

            def maxima(i, k):
                for g in range(G):
                    dve.wait_ge(scores_done, G * BPT * i + (G * k + g + 1))
                    dve.tensor_reduce(neg_max[k % 2][:, g:g + 1], s_bank[g][:, 0:SKV], AX.X, ALU.max,
                                      negate=True).then_inc(max_ready, 1)

            def turned(i, k, first=False):
                dve.wait_ge(pt_done, 2 * BPT * i + (2 * k + 1))
                if not (first and k < 2):
                    dve.wait_ge(pv_done, BPT * i + (k - 1))
                dve.tensor_copy(pt_sb[k % 2][:, 0, :], pt_bank[0][:]).then_inc(pt0_ready, 1)

            def take_output(i, k):
                dve.wait_ge(pv_done, BPT * i + (k + 1))
                for j in range(J):
                    src = diagonal(o_bank, j)
                    dst = att_tok[SQ * k:SQ * (k + 1), bass.ds(i, 1), :].rearrange(
                        "p t (g j d) -> p (t g) j d", g=G, j=J)[:, :, j, :]
                    last = dve.tensor_copy(dst, src)
                last.then_inc(o_taken, 1)

            def diagonal(tensor, j):
                ap = tensor[SQ * j:SQ * (j + 1), HD * j:HD * (j + 1)].copy()
                (row, p), (one, d) = ap.ap
                return bass.AP(ap.tensor, ap.offset, [[row, p], [128 + J * HD, G], [one, d]])

            def group(i, first=False, last=False):
                for k in range(BPT):
                    if first and k == 0:
                        maxima(0, 0)
                    turned(i, k, first)
                    if not (last and k == BPT - 1):
                        maxima(*((i, k + 1) if k < BPT - 1 else (i + 1, 0)))
                    take_output(i, k)

            group(0, first=True)
            with dve.Fori(1, B // BPT - 1) as i:
                group(i)
            group(B // BPT - 1, last=True)

            dve.wait_ge(last_kept, B)
            for j in range(J):
                for k in range(BPT):
                    src = sum_last[SQ * j:SQ * (j + 1), :, :, :].rearrange(
                        "p s (t k) g -> p s t k g", k=BPT)[:, :, :, k, :]
                    dst = sum_last_tok[SQ * k:SQ * (k + 1), :, :, :].rearrange(
                        "p s t (g j) -> p s t g j", j=J)[:, :, :, :, j]
                    last = dve.tensor_copy(dst, src)
            own(last)
            heads = [128, NT, H, HD]
            att = att_tok[:].rearrange("p t (h d) -> p t h d", d=HD)
            vl = v_last[:].rearrange("p t (h d) -> p t h d", d=HD)
            dve.wait_ge(v_last_ready, 2)
            own(dve.reciprocal(r_sum[:], sum_last_tok[:, 0, :, :]))
            own(dve.tensor_tensor(vl, vl, sum_last_tok[:, 1, :, :].unsqueeze(3).to_broadcast(heads), ALU.mult))
            own(dve.tensor_tensor(att, att, vl, ALU.add))
            own(dve.tensor_tensor(att, att, r_sum[:].unsqueeze(3).to_broadcast(heads), ALU.mult))
            dve.wait_ge(row_in, 16)
            dve.tensor_tensor(att_tok[:], att_tok[:], row_sb[:, 0, :].unsqueeze(1).to_broadcast([128, NT, D]),
                              ALU.add).then_inc(att_ready, 1)
            dve.wait_ge(xbo_ready, 1)
            dve.wait_ge(wo_done, 1)
            for n in range(2):
                part = x1_tok[:, 4 * n:4 * n + 4, :].rearrange("p t d -> p (t d)")
                last = dve.tensor_tensor(part, bank[n][:], part, ALU.add)
            own(last)
            layer_norm(x1_tok, 2)
            dve.wait_ge(norm_turned, 3)
            dve.tensor_copy(norm_ft[:, 0:HALF], bank[4][:]).then_inc(norm_ft_ready, 1)
            for n in range(2):
                dve.wait_ge(mix_done, 3 + n)
                last = dve.tensor_copy(xb_ft[:, 16 * n:16 * n + 16, 0:SQ - 1],
                                       bank[2 + n][:].rearrange("p (b q) -> p b q", q=SQ)[:, :, 1:SQ])
            own(last)
            dve.wait_ge(xf_ready, 2)
            dve.wait_ge(edges_ready, 2)
            dve.tensor_tensor(s_ft[:].rearrange("p (b q) -> p b q", q=SQ), xf_ft[:], xb_ft[:],
                              ALU.add).then_inc(s_ready, 1)
            dve.wait_ge(gamma_ready, 1)
            dve.wait_ge(mix2_done, 2)
            for n in range(2):
                part = slice(4 * n, 4 * n + 4)
                last = dve.tensor_tensor(x2_tok[:, part, :].rearrange("p t d -> p (t d)"), bank[4 + n][:],
                                         norm_tok[:, part, :].rearrange("p t d -> p (t d)"), ALU.subtract)
            own(last)
            for t in range(NT):
                last = dve.scalar_tensor_tensor(out=x2_tok[:, t, :], in0=x2_tok[:, t, :],
                                                scalar=gamma[:, t:t + 1], in1=norm_tok[:, t, :],
                                                op0=ALU.mult, op1=ALU.add)
            own(last)
            own(dve.tensor_tensor(x2_tok[:], x2_tok[:], x1_tok[:], ALU.add))
            layer_norm(x2_tok, 3)
            dve.wait_ge(norm_turned, 5)
            dve.tensor_copy(norm_ft[:, 0:HALF], bank[4][:]).then_inc(norm_ft_ready, 1)
            dve.wait_ge(logits_done, 1)
            own(dve.tensor_copy(logits[:].rearrange("p t e -> p (t e)"), bank[7][:, 0:NT * E]))
            for t in range(NT):
                last = dve.max(top[:, t, :], logits[:, t, :])
            own(last)
            dve.tensor_tensor(top_d[:], top[:, :, 0], top[:, :, 1], ALU.subtract).then_inc(top_ready, 1)
            for t in range(NT):
                last = dve.max_index(top_at[:, t, :], top[:, t, :], logits[:, t, :])
            own(last)
            own(dve.tensor_copy(top_no[:], top_at[:, :, 0:2]))
            dve.wait_ge(consts_ready, 2)
            dve.wait_ge(top_w_ready, 2)
            te = [128, NT, E]
            for n in range(2):
                last = dve.tensor_tensor(pick[:, n, :, :], expert_no[:].unsqueeze(1).to_broadcast(te),
                                         top_no[:, :, n:n + 1].to_broadcast(te), ALU.is_equal)
            own(last)
            for n in range(2):
                last = dve.tensor_tensor(pick[:, n, :, :], pick[:, n, :, :],
                                         top_w[:, :, n:n + 1].to_broadcast(te), ALU.mult)
            own(last)
            own(dve.tensor_tensor(share[:], pick[:, 0, :, :], pick[:, 1, :, :], ALU.add))

            def gated(i, n, h, first=False):
                for c in range(FC):
                    at = 2 * FC * n + FC * h + c
                    dve.wait_ge(silu_ready, 16 * i + (at + 1))
                    if c == 0 and not (first and n == 0):
                        dve.wait_ge(y_done, 4 * i + (2 * n + h - 1))
                    dve.tensor_tensor(hid_sb[h][:, c, :], silu_sb[at % 2][:], bank[2 + at % 2][:],
                                      ALU.mult).then_inc(hid_ready, 1)

            def add_share(i, n, h, first=False):
                at = 2 * n + h
                dve.wait_ge(y_done, 4 * i + (at + 1))
                if not (first and at < 2):
                    dve.wait_ge(y_added, 4 * i + (at - 1))
                for t in range(4):
                    last = dve.scalar_tensor_tensor(
                        out=x2_tok[:, 4 * h + t, :], in0=bank[6 + h][:, tile(t)],
                        scalar=share[:, 4 * h + t, bass.ds(2 * i + n, 1)], in1=x2_tok[:, 4 * h + t, :],
                        op0=ALU.mult, op1=ALU.add)
                last.then_inc(y_added, 1)

            def two_experts(i, first=False):
                gated(i, 0, 0, first)
                if not first:
                    add_share(i - 1, 1, 1)
                gated(i, 0, 1, first)
                add_share(i, 0, 0, first)
                gated(i, 1, 0)
                add_share(i, 0, 1, first)
                gated(i, 1, 1)
                add_share(i, 1, 0)

            two_experts(0, True)
            with dve.Fori(1, E // 2) as i:
                two_experts(i)
            add_share(E // 2 - 1, 1, 1)


def kernel(**inputs):
    import numpy as np
    import concourse.bacc as bacc
    from concourse.bass_utils import run_bass_kernel_spmd

    a = {name: np.asarray(value) for name, value in inputs.items()}
    ctx = a["ctx_1024"].transpose(2, 0, 1)
    arrays = {
        "x": a["x"].reshape(TOK, D),
        "ctx_keys": ctx[:, :, 0:KEYS],
        "ctx_last": ctx[:, :, KEYS],
        "weights": np.concatenate([a["L0_xattn_wq"].T, a["L0_xattn_wk"].T, a["L0_xattn_wv"].T,
                                   a["L0_xattn_wo"].T, a["L0_attn_WB"].T, a["L0_attn_WBf"].T], axis=1),
        "vectors": np.stack([a["L0_xattn_bq"], a["L0_xattn_bk"], a["L0_attn_w1"][0], a["L0_attn_w2"][0],
                             np.broadcast_to(a["L0_attn_b"], (D,))], axis=1),
        "rows": np.stack([a["L0_xattn_bv"], a["L0_xattn_bo"]]),
        "gate": a["L0_ffn_gate_kernel"],
        "w01": np.stack([a["L0_ffn_w0"], a["L0_ffn_w1"]], axis=2),
        "wo": a["L0_ffn_wo"].reshape(E, FC, 128, D).transpose(0, 2, 1, 3),
    }
    arrays = {name: np.ascontiguousarray(value) for name, value in arrays.items()}
    nc = bacc.Bacc("TRN2", target_bir_lowering=False, num_devices=1)
    args = [nc.dram_tensor(name, v.shape, mybir.dt.from_np(v.dtype), kind="ExternalInput").ap()
            for name, v in arrays.items()]
    out = nc.dram_tensor("out", (TOK, D), F32, kind="ExternalOutput").ap()
    build(nc, *args, out)
    result = run_bass_kernel_spmd(nc, [arrays], core_ids=[0])
    return result.results[0]["out"].reshape(B, SQ, D)
```

```python
from contextlib import ExitStack

import concourse.bass as bass
from concourse import mybir

F32 = mybir.dt.float32
F32R = mybir.dt.float32r
BF16 = mybir.dt.bfloat16
I32 = mybir.dt.int32
U32 = mybir.dt.uint32
ALU = mybir.AluOpType
ACT = mybir.ActivationFunctionType
AX = mybir.AxisListType

B, SQ, D = 32, 32, 128
SKV = 257
SKP = 258
HF = D // 2
KEYS = 256
H, HD = 16, 8
G, J = 4, 4
TOK = B * SQ
NT = TOK // 128
BPT = 128 // SQ
E, F, FC = 8, 512, 4
HALF = TOK // 2
TOPK = 2
SLOT_TILES = (TOPK * TOK + E * 127) // 128
SLOT_EVEN = SLOT_TILES + SLOT_TILES % 2
SLOT_BUFS = 4
TABLE_ROWS = TOPK * TOK
ROW = D + 2
EPS = 1e-5
Q_SCALE = float(HD) ** -0.5

W_Q0, W_Q1, W_K, W_V, W_O, W_B, W_BF = (slice(n * D, (n + 1) * D) for n in range(7))
V_BQ0, V_BQ1, V_BK, V_W1, V_W2, V_B = (slice(n, n + 1) for n in range(6))


def build(nc, x, ctx_keys, ctx_last, weights, vectors, rows, gate, w01, wo, out):
    with ExitStack() as stack:
        def sb(name, shape, dt=F32):
            return stack.enter_context(nc.sbuf_tensor(name, shape, dt))

        def sem(name):
            return stack.enter_context(nc.semaphore(name))

        x_tok = sb("x_tok", [128, NT, D])
        x1_tok = sb("x1_tok", [128, NT, D])
        x2_tok = sb("x2_tok", [128, NT, D])
        w_sb = sb("w_sb", [128, 7 * D])
        vec_sb = sb("vec_sb", [128, 6])
        row_sb = sb("row_sb", [128, 2, D])
        gate_sb = sb("gate_sb", [128, E])
        last_sb = sb("last_sb", [128, B])
        last_rep = sb("last_rep", [128, B, SQ])
        ident = sb("ident", [128, 128])
        head_mask = sb("head_mask", [128, H // 2])
        expert_no = sb("expert_no", [128, E])
        norm_tok = sb("norm_tok", [128, NT, D])
        norm_ft = sb("norm_ft", [128, TOK])
        stats = sb("stats", [128, NT, 6])
        mean_var = sb("mean_var", [128, NT, 2])
        var_eps = sb("var_eps", [128, NT])
        minus_half = sb("minus_half", [128, NT])
        rstd = sb("rstd", [128, NT])
        q_twice = sb("q_twice", [128, 2, TOK])
        q_now = [sb(f"q_now{n}", [128, 2, SQ]) for n in range(2)]
        q_parts = [sb(f"q_parts{n}", [128, 2, 2, SQ], F32R) for n in range(2)]
        k_last = sb("k_last", [128, B])
        k_last_split = sb("k_last_split", [128, 2, B, 2], F32R)
        v_last = sb("v_last", [128, NT, D])
        ctx_sb = [sb(f"ctx_sb{n}", [128, KEYS]) for n in range(BPT)]
        k_sb = [sb(f"k_sb{n}", [128, KEYS]) for n in range(2)]
        k_split = [sb(f"k_split{n}", [128, 2, SKP], F32R) for n in range(2)]
        v_sb = [sb(f"v_sb{n}", [128, 2, D]) for n in range(BPT)]
        qbd_sb = [sb(f"qbd_sb{n}", [128, 4, H // 2, SQ], F32R) for n in range(2)]
        neg_max = [sb(f"neg_max{n}", [128, G]) for n in range(2)]
        p_sb = [sb(f"p_sb{n}", [128, G, SKV]) for n in range(2)]
        pt_sb = [sb(f"pt_sb{n}", [128, 2, G * 128]) for n in range(2)]
        sum_last = sb("sum_last", [128, 2, B, G])
        sum_last_tok = sb("sum_last_tok", [128, 2, NT, H])
        r_sum = sb("r_sum", [128, NT, H])
        att_tok = sb("att_tok", [128, NT, D])
        att_ft = sb("att_ft", [128, TOK])
        xf_ft = sb("xf_ft", [128, B, SQ])
        xb_ft = sb("xb_ft", [128, B, SQ])
        s_ft = sb("s_ft", [128, TOK])
        gamma = sb("gamma", [128, NT])
        logits = sb("logits", [128, NT, E])
        top = sb("top", [128, NT, 8])
        top_at = sb("top_at", [128, NT, 8], U32)
        top_no = sb("top_no", [128, NT, 2])
        top_d = sb("top_d", [128, NT])
        pick = sb("pick", [128, TOPK, NT, E])
        chosen = sb("chosen", [128, NT, E], BF16)
        before = sb("before", [128, 128], BF16)
        ones = sb("ones", [128, 128], BF16)
        expert_before = sb("expert_before", [128, E, E])
        tile_starts = sb("tile_starts", [128, E])
        tile_no = sb("tile_no", [128, SLOT_EVEN])
        square = sb("square", [128, E, E])
        n_tiles = sb("n_tiles", [128, E])
        first_tile = sb("first_tile", [128, E])
        end_tile = sb("end_tile", [128, E])
        slot = sb("slot", [128, NT, E])
        slot_of = sb("slot_of", [128, TOPK, NT])
        slot_at = sb("slot_at", [128, TOPK, NT], U32)
        slot_tile = sb("slot_tile", [128, TOPK, NT], U32)
        slot_in_tile = sb("slot_in_tile", [128, TOPK, NT], U32)
        row_back = sb("row_back", [128, TOPK, NT])
        slot_nos = sb("slot_nos", [128, 128])
        in_tile = sb("in_tile", [128, TOPK, NT, SLOT_EVEN])
        row_in_tile = sb("row_in_tile", [128, TOPK * NT, SLOT_EVEN], F32R)
        at_slot = sb("at_slot", [128, TOPK * NT, 128], F32R)
        slot_row = sb("slot_row", [128, SLOT_TILES], U32)
        tile_after = sb("tile_after", [1, SLOT_TILES, E])
        tile_expert_f = sb("tile_expert_f", [1, SLOT_TILES])
        tile_expert = sb("tile_expert", [1, SLOT_TILES], I32)
        rows_tok = sb("rows_tok", [128, NT, TOPK, ROW])
        empty_row = sb("empty_row", [128, ROW])
        w01_sb = sb("w01_sb", [128, E, 2, F])
        wo_sb = sb("wo_sb", [128, E, FC, D])
        slot_sb = [sb(f"slot_sb{n}", [128, ROW]) for n in range(SLOT_BUFS)]
        slot_meta = sb("slot_meta", [128, SLOT_TILES, 2])
        slot_ft = [sb(f"slot_ft{n}", [128, 128]) for n in range(2)]
        silu_sb = [sb(f"silu_sb{n}", [128, F]) for n in range(2)]
        hid_sb = [sb(f"hid_sb{n}", [128, F]) for n in range(2)]
        hid_ft = [sb(f"hid_ft{n}", [128, FC, 128]) for n in range(2)]
        y_sb = [sb(f"y_sb{n}", [128, D]) for n in range(2)]
        y_tok = [sb(f"y_tok{n}", [128, 1], U32) for n in range(2)]
        table = nc.dram_tensor("table", (TABLE_ROWS + 1, ROW), F32).ap()

        bank = [stack.enter_context(nc.psum_tensor(f"bank{n}", [128, 512], F32)) for n in range(8)]
        s_bank = bank[0:4]
        pt_bank = bank[4:6]
        kv_bank = bank[6]
        o_bank = bank[7]

        x_in, w_in, vec_in, row_in, gate_in, last_in = (
            sem(n) for n in ("x_in", "w_in", "vec_in", "row_in", "gate_in", "last_in"))
        ctx_in = [sem(f"ctx_in{n}") for n in range(BPT)]
        expert_in, table_stored, out_started = (sem(n) for n in ("expert_in", "table_stored", "out_started"))
        slot_in = [sem(f"slot_in{n}") for n in range(SLOT_BUFS)]
        out_done = sem("out_done")
        kv_done, k_ready, kl_split_ready, k_last_ready, v_ready, q_parts_ready, qbd_ready = (
            sem(n) for n in ("kv_done", "k_ready", "kl_split_ready", "k_last_ready", "v_ready", "q_parts_ready", "qbd_ready"))
        k_high_ready, k_split_ready = sem("k_high_ready"), sem("k_split_ready")
        scores_done, max_ready, probs_ready, pt_done, pt0_ready, pt1_ready = (
            sem(n) for n in ("scores_done", "max_ready", "probs_ready", "pt_done", "pt0_ready", "pt1_ready"))
        last_kept, pv_done, o_taken = (sem(n) for n in ("last_kept", "pv_done", "o_taken"))
        slot_turned, slot_ft_ready, gate_half_done, up_half_done, silu_ready, hid_ready = (
            sem(n) for n in ("slot_turned", "slot_ft_ready", "gate_half_done", "up_half_done",
                             "silu_ready", "hid_ready"))
        meta_kept = sem("meta_kept")
        hid_turned, hid_ft_ready, y_done, y_ready = (
            sem(n) for n in ("hid_turned", "hid_ft_ready", "y_done", "y_ready"))
        pool_step, dve_step, act_step = sem("pool_step"), sem("dve_step"), sem("act_step")
        consts_ready, last_rep_ready, xbo_ready = (
            sem(n) for n in ("consts_ready", "last_rep_ready", "xbo_ready"))
        var_ready, rstd_ready, normed, norm_turned, norm_ft_ready = (
            sem(n) for n in ("var_ready", "rstd_ready", "normed", "norm_turned", "norm_ft_ready"))
        pre_done, q_ready, v_last_ready, kl_ready = (
            sem(n) for n in ("pre_done", "q_ready", "v_last_ready", "kl_ready"))
        att_ready, att_turned, att_ft_ready, wo_done = (
            sem(n) for n in ("att_ready", "att_turned", "att_ft_ready", "wo_done"))
        mix_done, xf_ready, edges_ready, s_ready, mix2_done, gamma_ready = (
            sem(n) for n in ("mix_done", "xf_ready", "edges_ready", "s_ready", "mix2_done", "gamma_ready"))
        logits_done, top_ready, top_w_ready, chosen_ready, ranks_done = (
            sem(n) for n in ("logits_done", "top_ready", "top_w_ready", "chosen_ready", "ranks_done"))
        empty_ready, twin_ready, tile_expert_ready, x2_ready = (
            sem(n) for n in ("empty_ready", "twin_ready", "tile_expert_ready", "x2_ready"))
        at_slot_ready, slot_row_done, slot_row_ready = (
            sem(n) for n in ("at_slot_ready", "slot_row_done", "slot_row_ready"))

        block = stack.enter_context(nc.Block())

        def tile(t):
            return slice(t * 128, (t + 1) * 128)

        def slot_loads(s):
            return 16 * (s // SLOT_BUFS + 1)

        @block.sync
        def _(sp):
            sp.dma_start(x_tok[:], x.rearrange("(t p) d -> p t d", p=128)).then_inc(x_in, 16)
            sp.dma_start(w_sb[:], weights).then_inc(w_in, 16)
            sp.dma_start(vec_sb[:], vectors).then_inc(vec_in, 16)
            sp.dma_start(last_sb[:], ctx_last).then_inc(last_in, 16)
            for k in range(BPT):
                sp.dma_start(ctx_sb[k][:], ctx_keys[:, k, :]).then_inc(ctx_in[k], 16)
            sp.dma_start(row_sb[:], rows.partition_broadcast(128)).then_inc(row_in, 16)
            sp.dma_start(gate_sb[:], gate).then_inc(gate_in, 16)
            sp.wait_ge(empty_ready, 1)
            sp.dma_start(table[TABLE_ROWS:TABLE_ROWS + 1, :], empty_row[0:1, :]).then_inc(table_stored, 16)
            sp.dma_start(w01_sb[:, 0, :, :], w01[0]).then_inc(expert_in, 16)
            sp.dma_start(wo_sb[:, 0, :, :], wo[0]).then_inc(expert_in, 16)
            with sp.Fori(1, B // BPT) as i:
                for k in range(BPT):
                    sp.wait_ge(kv_done, BPT * i + (k - BPT + 1))
                    sp.dma_start(ctx_sb[k][:], ctx_keys[:, BPT * i + k, :]).then_inc(ctx_in[k], 16)
                sp.dma_start(w01_sb[:, bass.ds(i, 1), :, :].rearrange("p e m f -> p (e m f)"),
                             w01[bass.ds(i, 1)].rearrange("e p m f -> p (e m f)")).then_inc(expert_in, 16)
                sp.dma_start(wo_sb[:, bass.ds(i, 1), :, :].rearrange("p e c d -> p (e c d)"),
                             wo[bass.ds(i, 1)].rearrange("e p c d -> p (e c d)")).then_inc(expert_in, 16)
            sp.wait_ge(x2_ready, 1)
            sp.dma_start(out.rearrange("(t p) d -> p t d", p=128), x2_tok[:]).then_inc(out_started, 16)

            for c in range(TOPK):
                if c == 1:
                    sp.wait_ge(twin_ready, 1)
                sp.wait_ge(top_w_ready, c + 1)
                sp.dma_start(table[TOK * c:TOK * (c + 1), :].rearrange("(t p) r -> p t r", p=128),
                             rows_tok[:, :, c, :]).then_inc(table_stored, 16)
            sp.wait_ge(out_done, 16 * SLOT_TILES)

        @block.gpsimd
        def _(pool):
            steps = [0]

            def own(ins):
                steps[0] += 1
                ins.then_inc(pool_step, 1)
                pool.wait_ge(pool_step, steps[0])

            def inverse_root(nth):
                pool.wait_ge(var_ready, nth)
                pool.tensor_tensor(rstd[:], var_eps[:], minus_half[:], ALU.pow).then_inc(rstd_ready, 1)

            own(pool.memset(minus_half[:], -0.5))
            inverse_root(1)
            own(pool.memset(ident[:], 0.0))
            pool.affine_select(out=ident[:], in_=ident[:], compare_op=ALU.not_equal, fill=1.0, base=0,
                               pattern=[[-1, 128]], channel_multiplier=1).then_inc(consts_ready, 1)
            own(pool.memset(head_mask[:], 1.0))
            for h in range(2):
                rows_h = head_mask[HF * h:HF * (h + 1), :]
                own(pool.affine_select(out=rows_h, in_=rows_h, compare_op=ALU.is_ge, fill=0.0,
                                       base=0, pattern=[[-HD, H // 2]], channel_multiplier=1))
                own(pool.affine_select(out=rows_h, in_=rows_h, compare_op=ALU.is_ge, fill=0.0,
                                       base=HD - 1, pattern=[[HD, H // 2]], channel_multiplier=-1))
            pool.wait_ge(last_in, 16)
            pool.tensor_copy(last_rep[:], last_sb[:].unsqueeze(2).to_broadcast([128, B, SQ])
                             ).then_inc(last_rep_ready, 1)
            pool.iota(expert_no[:], [[1, E]], base=0, channel_multiplier=0,
                      allow_small_or_imprecise_dtypes=True).then_inc(consts_ready, 1)
            own(pool.memset(empty_row[:], 0.0))
            pool.memset(empty_row[:, D + 1:ROW], float(TOK)).then_inc(empty_ready, 1)
            pool.iota(rows_tok[:, :, :, D + 1], [[128, NT], [0, TOPK]], base=0, channel_multiplier=1,
                      allow_small_or_imprecise_dtypes=True).then_inc(consts_ready, 1)
            pool.iota(tile_starts[:], [[128, E]], base=0, channel_multiplier=0,
                      allow_small_or_imprecise_dtypes=True).then_inc(consts_ready, 1)
            pool.iota(tile_no[:], [[1, SLOT_EVEN]], base=0, channel_multiplier=0,
                      allow_small_or_imprecise_dtypes=True).then_inc(consts_ready, 1)
            pool.iota(row_back[:], [[-TOK, TOPK], [-128, NT]], base=TABLE_ROWS, channel_multiplier=-1,
                      allow_small_or_imprecise_dtypes=True).then_inc(consts_ready, 1)
            pool.iota(slot_nos[:], [[1, 128]], base=0, channel_multiplier=0,
                      allow_small_or_imprecise_dtypes=True).then_inc(consts_ready, 1)
            pool.memset(ones[:], 1.0).then_inc(consts_ready, 1)
            own(pool.memset(before[:], 1.0))
            own(pool.memset(expert_before[:], 1.0))
            pool.affine_select(out=before[:], in_=before[:], compare_op=ALU.is_gt, fill=0.0, base=0,
                               pattern=[[1, 128]], channel_multiplier=-1).then_inc(consts_ready, 1)
            pool.affine_select(out=expert_before[:], in_=expert_before[:], compare_op=ALU.is_gt, fill=0.0,
                               base=0, pattern=[[1, E], [-1, E]], channel_multiplier=0).then_inc(consts_ready, 1)
            pool.wait_ge(q_ready, 1)
            pool.wait_ge(kl_split_ready, 1)

            def batch(i, k, first=False):
                p = k % 2
                if not (first and k < 2):
                    pool.wait_ge(scores_done, G * BPT * i + G * (k - 1))
                q = q_twice[:, :, bass.ds(SQ * BPT * i + SQ * k, SQ)]
                pool.tensor_copy(q_now[p][:], q)
                pool.tensor_copy(q_parts[p][:, 0, :, :], q).then_inc(q_parts_ready, 1)
                pool.wait_ge(q_parts_ready, 2 * BPT * i + (2 * k + 1))
                pool.tensor_tensor(q_parts[p][:, 1, :, :], q_now[p][:], q_parts[p][:, 0, :, :], ALU.subtract
                                   ).then_inc(q_parts_ready, 1)
                pool.wait_ge(q_parts_ready, 2 * BPT * i + (2 * k + 2))
                shape = [128, 4, H // 2, SQ]
                pool.tensor_tensor(qbd_sb[p][:],
                                   q_parts[p][:].rearrange("p s h q -> p (s h) q").unsqueeze(2).to_broadcast(shape),
                                   head_mask[:].unsqueeze(1).unsqueeze(3).to_broadcast(shape),
                                   ALU.mult).then_inc(qbd_ready, 1)
                pool.tensor_copy(k_split[p][:, :, KEYS:SKP], k_last_split[:, :, bass.ds(BPT * i + k, 1), :]
                                 .rearrange("p h a n -> p h (a n)")).then_inc(k_last_ready, 1)

            def keep_last(i, k):
                pool.wait_ge(probs_ready, G * BPT * i + G * (k + 1))
                pool.tensor_copy(sum_last[:, 1, bass.ds(BPT * i + k, 1), :].rearrange("p a g -> p (a g)"),
                                 p_sb[k % 2][:, :, KEYS]).then_inc(last_kept, 1)

            batch(0, 0, True)
            batch(0, 1, True)
            pool.wait_ge(q_ready, 2)
            for k in range(2, BPT):
                batch(0, k, True)
                keep_last(0, k - 2)
            with pool.Fori(1, B // BPT) as i:
                for k in range(BPT):
                    batch(i, k)
                    if k < 2:
                        keep_last(i - 1, k + 2)
                    else:
                        keep_last(i, k - 2)
            keep_last(B // BPT - 1, 2)
            keep_last(B // BPT - 1, 3)

            pool.wait_ge(row_in, 16)
            pool.wait_ge(x_in, 16)
            pool.tensor_tensor(x1_tok[:], x_tok[:], row_sb[:, 1, :].unsqueeze(1).to_broadcast([128, NT, D]),
                               ALU.add).then_inc(xbo_ready, 1)
            inverse_root(2)
            u = norm_ft[:].rearrange("p (b q) -> p b q", q=SQ)
            pool.wait_ge(norm_ft_ready, 4)
            pool.tensor_copy(xf_ft[:, :, 0:1], u[:, :, 0:1]).then_inc(edges_ready, 1)
            pool.tensor_copy(xb_ft[:, :, SQ - 1:SQ], u[:, :, SQ - 1:SQ]).then_inc(edges_ready, 1)
            inverse_root(3)
            pool.wait_ge(normed, 3)
            pool.tensor_copy(rows_tok[:, :, 1, 0:D], rows_tok[:, :, 0, 0:D]).then_inc(twin_ready, 1)

            def gather(s):
                pool.indirect_dma_start(slot_sb[s % SLOT_BUFS][:], None, table,
                                        bass.IndirectOffsetOnAxis(slot_row[:, s:s + 1], 0)
                                        ).then_inc(slot_in[s % SLOT_BUFS], 16)

            pool.wait_ge(table_stored, 16 * (TOPK + 1))
            pool.wait_ge(slot_row_ready, 1)
            for s in range(SLOT_BUFS):
                gather(s)
            last_token = pool.to_reg(TOK - 1)
            for s in range(SLOT_TILES):
                pool.wait_ge(y_ready, s + 1)
                if s == 0:
                    pool.wait_ge(out_started, 16)
                else:
                    pool.wait_ge(out_done, 16 * s)
                pool.indirect_dma_start(
                    out, bass.IndirectOffsetOnAxis(y_tok[s % 2][:], 0), y_sb[s % 2][:], None,
                    bounds_check=last_token, oob_is_err=False, compute_op=ALU.add).then_inc(out_done, 16)
                if s + SLOT_BUFS < SLOT_TILES:
                    pool.wait_ge(slot_turned, s + 1)
                    pool.wait_ge(meta_kept, s + 1)
                    gather(s + SLOT_BUFS)

        @block.scalar
        def _(act):
            act.wait_ge(vec_in, 16)
            act.wait_ge(pre_done, 2)
            act.activation(k_last[:], kv_bank[:, 0:B], ACT.Identity, bias=vec_sb[:, V_BK]).then_inc(kl_ready, 1)
            for n in range(2):
                act.activation(v_last[:, 4 * n:4 * n + 4, :].rearrange("p t d -> p (t d)"), bank[2 + n][:],
                               ACT.Copy).then_inc(v_last_ready, 1)

            def keys_values(i, k, first=False):
                act.wait_ge(kv_done, BPT * i + (k + 1))
                if not (first and k < 2):
                    act.wait_ge(k_split_ready, BPT * i + (k - 1))
                act.activation(k_sb[k % 2][:, 0:KEYS], kv_bank[:, 0:KEYS], ACT.Identity,
                               bias=vec_sb[:, V_BK]).then_inc(k_ready, 1)
                if not first:
                    act.wait_ge(pv_done, BPT * i + (k - BPT + 1))
                act.activation(v_sb[k][:].rearrange("p t d -> p (t d)"), kv_bank[:, KEYS:512],
                               ACT.Copy).then_inc(v_ready, 1)

            def softmax(i, k, first=False):
                p = k % 2
                if not (first and k < 2):
                    act.wait_ge(pt_done, 2 * BPT * i + 2 * (k - 1))
                    act.wait_ge(last_kept, BPT * i + (k - 1))
                for g in range(G):
                    act.wait_ge(max_ready, G * BPT * i + (G * k + g + 1))
                    act.activation(p_sb[p][:, g, :], s_bank[g][:, 0:SKV], ACT.Exp, bias=neg_max[p][:, g:g + 1],
                                   accum_out=sum_last[:, 0, bass.ds(BPT * i + k, 1), g]
                                   ).then_inc(probs_ready, 1)

            def turned(i, k, first=False):
                act.wait_ge(pt_done, 2 * BPT * i + 2 * (k + 1))
                if not (first and k < 2):
                    act.wait_ge(pv_done, BPT * i + (k - 1))
                act.activation(pt_sb[k % 2][:, 1, :], pt_bank[1][:], ACT.Copy).then_inc(pt1_ready, 1)

            def group(i, first=False, last=False):
                for k in range(BPT):
                    if first and k == 0:
                        keys_values(i, 0, True)
                        keys_values(i, 1, True)
                    softmax(i, k, first)
                    if k < 2:
                        keys_values(i, k + 2, first)
                    elif not last:
                        keys_values(i + 1, k - 2)
                    turned(i, k, first)

            group(0, first=True)
            with act.Fori(1, B // BPT - 1) as i:
                group(i)
            group(B // BPT - 1, last=True)

            for n in range(2):
                act.wait_ge(att_turned, n + 1)
                act.activation(att_ft[:, n * HALF:(n + 1) * HALF], bank[4 + n][:], ACT.Copy).then_inc(att_ft_ready, 1)
            act.wait_ge(norm_turned, 4)
            act.activation(norm_ft[:, HALF:TOK], bank[5][:], ACT.Copy).then_inc(norm_ft_ready, 1)
            for n in range(2):
                act.wait_ge(mix_done, n + 1)
                act.activation(xf_ft[:, 16 * n:16 * n + 16, 1:SQ],
                               bank[n][:].rearrange("p (b q) -> p b q", q=SQ)[:, :, 1:SQ],
                               ACT.Copy).then_inc(xf_ready, 1)
            act.wait_ge(mix2_done, 1)
            act.activation(gamma[:], bank[6][:, 0:NT], ACT.Sigmoid, bias=vec_sb[:, V_B]).then_inc(gamma_ready, 1)
            act.wait_ge(norm_turned, 6)
            act.activation(norm_ft[:, HALF:TOK], bank[5][:], ACT.Copy).then_inc(norm_ft_ready, 1)
            act.wait_ge(top_ready, 1)
            for c in range(TOPK):
                act.activation(rows_tok[:, :, c, D], top_d[:], ACT.Sigmoid,
                               scale=1.0 - 2.0 * c).then_inc(top_w_ready, 1)

            def slot_features(s):
                act.wait_ge(slot_turned, s + 1)
                if s >= 2:
                    act.wait_ge(up_half_done, s - 1)
                act.activation(slot_ft[s % 2][:], bank[7][:, 0:128], ACT.Copy).then_inc(slot_ft_ready, 1)

            slot_features(0)
            for s in range(SLOT_TILES):
                if s + 1 < SLOT_TILES:
                    slot_features(s + 1)
                act.wait_ge(gate_half_done, s + 1)
                if s >= 2:
                    act.wait_ge(hid_ready, s - 1)
                act.activation(silu_sb[s % 2][:], bank[s % 2][:], ACT.Silu).then_inc(silu_ready, 1)

        @block.tensor
        def _(pe):
            def turn(src, dst_banks, count_sem):
                for n in range(2):
                    for t in range(4):
                        last = pe.transpose(dst_banks[n][:, tile(t)], src[:, 4 * n + t, :], ident[:])
                    last.then_inc(count_sem, 1)

            pe.wait_ge(last_in, 16)
            pe.wait_ge(w_in, 16)
            pe.wait_ge(last_rep_ready, 1)
            pe.matmul(kv_bank[:, 0:B], w_sb[:, W_K], last_sb[:], start=True, stop=True)
            for t in range(NT):
                last = pe.matmul(bank[2 + t // 4][:, tile(t % 4)],
                                 last_rep[:, BPT * t:BPT * (t + 1), :].rearrange("p b q -> p (b q)"),
                                 w_sb[:, W_V], start=True, stop=True)
            last.then_inc(pre_done, 2)
            pe.wait_ge(consts_ready, 1)
            pe.wait_ge(normed, 1)
            turn(norm_tok, bank[4:6], norm_turned)
            for n in range(2):
                pe.wait_ge(norm_ft_ready, n + 1)
                if n == 1:
                    pe.wait_ge(v_last_ready, 2)
                for h in range(2):
                    pe.matmul(bank[2 * n + h][:], w_sb[:, (W_Q0, W_Q1)[h]], norm_ft[:, n * HALF:(n + 1) * HALF],
                              start=True, stop=True).then_inc(pre_done, 1)

            def keys_values(i, k, first=False):
                if first and k == 0:
                    pe.wait_ge(kl_ready, 1)
                else:
                    pe.wait_ge(k_ready, BPT * i + k)
                    pe.wait_ge(v_ready, BPT * i + k)
                pe.wait_ge(ctx_in[k], 16 * i + 16)
                pe.matmul(kv_bank[:, 0:KEYS], w_sb[:, W_K], ctx_sb[k][:], start=True, stop=True)
                for t in range(2):
                    last = pe.matmul(kv_bank[:, KEYS + 128 * t:KEYS + 128 * (t + 1)], ctx_sb[k][:, tile(t)],
                                     w_sb[:, W_V], start=True, stop=True)
                last.then_inc(kv_done, 1)

            def scores(i, k, first=False):
                pe.wait_ge(k_split_ready, BPT * i + (k + 1))
                pe.wait_ge(k_last_ready, BPT * i + (k + 1))
                pe.wait_ge(qbd_ready, BPT * i + (k + 1))
                for g in range(G):
                    if first and k == 0:
                        if g == 0:
                            pe.wait_ge(q_ready, 2)
                    else:
                        pe.wait_ge(probs_ready, G * BPT * i + (G * (k - 1) + g + 1))
                    half, heads = g // 2, slice(J * (g % 2), J * (g % 2 + 1))
                    for part in range(2):
                        last = pe.matmul(s_bank[g][:, 0:SKP],
                                         qbd_sb[k % 2][:, 2 * part + half, heads, :].rearrange("p h q -> p (h q)"),
                                         k_split[k % 2][:, half, :], start=(part == 0), stop=(part == 1))
                    last.then_inc(scores_done, 1)

            def turn_probs(i, k, first=False):
                pe.wait_ge(probs_ready, G * BPT * i + G * (k + 1))
                for t in range(2):
                    if not (first and k == 0):
                        pe.wait_ge((pt0_ready, pt1_ready)[t], BPT * i + k)
                    for g in range(G):
                        last = pe.transpose(pt_bank[t][:, tile(g)], p_sb[k % 2][:, g, tile(t)], ident[:])
                    last.then_inc(pt_done, 1)

            def weigh_values(i, k, first=False):
                pe.wait_ge(v_ready, BPT * i + (k + 1))
                pe.wait_ge(pt0_ready, BPT * i + (k + 1))
                pe.wait_ge(pt1_ready, BPT * i + (k + 1))
                if not (first and k == 0):
                    pe.wait_ge(o_taken, BPT * i + k)
                for g in range(G):
                    for t in range(2):
                        last = pe.matmul(o_bank[:, tile(g)], pt_sb[k % 2][:, t, tile(g)], v_sb[k][:, t, :],
                                         start=(t == 0), stop=(t == 1))
                last.then_inc(pv_done, 1)

            def group(i, first=False, last=False):
                for k in range(BPT):
                    more = not (last and k == BPT - 1)
                    after = (i, k + 1) if k < BPT - 1 else (i + 1, 0)
                    turn_probs(i, k, first)
                    if more:
                        scores(*after)
                    if k == 0:
                        keys_values(i, 3)
                    elif not last:
                        keys_values(i + 1, k - 1)
                    weigh_values(i, k, first)

            keys_values(0, 0, True)
            keys_values(0, 1)
            scores(0, 0, True)
            keys_values(0, 2)
            group(0, first=True)
            with pe.Fori(1, B // BPT - 1) as i:
                group(i)
            group(B // BPT - 1, last=True)

            pe.wait_ge(att_ready, 1)
            turn(att_tok, bank[4:6], att_turned)
            for t in range(NT):
                if t % 4 == 0:
                    pe.wait_ge(att_ft_ready, t // 4 + 1)
                last = pe.matmul(bank[t // 4][:, tile(t % 4)], att_ft[:, tile(t)], w_sb[:, W_O],
                                 start=True, stop=True)
            last.then_inc(wo_done, 1)
            pe.wait_ge(normed, 2)
            turn(norm_tok, bank[4:6], norm_turned)
            pe.wait_ge(norm_ft_ready, 4)
            for m in range(2):
                for n in range(2):
                    pe.matmul(bank[2 * m + n][:], w_sb[:, (W_B, W_BF)[m]], norm_ft[:, n * HALF:(n + 1) * HALF],
                              start=True, stop=True).then_inc(mix_done, 1)
            pe.wait_ge(xf_ready, 2)
            pe.wait_ge(s_ready, 1)
            for t in range(NT):
                for m, part in enumerate((xf_ft, xb_ft)):
                    last = pe.matmul(bank[6][:, t:t + 1],
                                     part[:, BPT * t:BPT * (t + 1), :].rearrange("p b q -> p (b q)"),
                                     vec_sb[:, (V_W1, V_W2)[m]], start=(m == 0), stop=(m == 1))
            last.then_inc(mix2_done, 1)
            for n in range(2):
                for t in range(4):
                    last = pe.transpose(bank[4 + n][:, tile(t)], s_ft[:, tile(4 * n + t)], ident[:])
            last.then_inc(mix2_done, 1)
            pe.wait_ge(normed, 3)
            turn(rows_tok[:, :, 0, 0:D], bank[4:6], norm_turned)
            pe.wait_ge(norm_ft_ready, 6)
            pe.wait_ge(gate_in, 16)
            for t in range(NT):
                last = pe.matmul(bank[7][:, E * t:E * (t + 1)], norm_ft[:, tile(t)], gate_sb[:],
                                 start=True, stop=True)
            last.then_inc(logits_done, 1)

            pe.wait_ge(chosen_ready, 1)
            pe.wait_ge(consts_ready, 10)
            pe.matmul(bank[6][:, 0:NT * E], before[:], chosen[:].rearrange("p t e -> p (t e)"),
                      start=True, stop=False, skip_group_check=True)
            for t in range(1, NT):
                last = pe.matmul(bank[6][:, t * E:NT * E], ones[:],
                                 chosen[:, 0:NT - t, :].rearrange("p t e -> p (t e)"),
                                 start=False, stop=(t == NT - 1), skip_group_check=True)
            last.then_inc(ranks_done, 1)
            for t in range(NT):
                last = pe.matmul(bank[7][:, 128:128 + E], ones[:], chosen[:, t, :], start=(t == 0),
                                 stop=(t == NT - 1))
            last.then_inc(ranks_done, 1)

            for n in range(TOPK * NT):
                if n % NT == 0:
                    pe.wait_ge(at_slot_ready, n // NT + 1)
                last = pe.matmul(bank[3][:, 0:SLOT_EVEN], at_slot[:, n, :], row_in_tile[:, n, :],
                                 start=(n == 0), stop=(n == TOPK * NT - 1))
            last.then_inc(slot_row_done, 1)

            def turn_slots(s):
                pe.wait_ge(slot_in[s % SLOT_BUFS], slot_loads(s))
                if s >= 1:
                    pe.wait_ge(slot_ft_ready, s)
                pe.transpose(bank[7][:, 0:128], slot_sb[s % SLOT_BUFS][:, 0:D], ident[:]).then_inc(slot_turned, 1)

            def half_hidden(s, m):
                if m == 0:
                    pe.wait_ge(slot_ft_ready, s + 1)
                if s >= 2:
                    pe.wait_ge((silu_ready, hid_ready)[m], s - 1)
                pe.matmul(bank[2 * m + s % 2][:], slot_ft[s % 2][:],
                          w01_sb[:, bass.ds(expert[s], 1), m, :].rearrange("p e f -> p (e f)"),
                          start=True, stop=True).then_inc((gate_half_done, up_half_done)[m], 1)

            def turn_hidden(s):
                pe.wait_ge(hid_ready, s + 1)
                if s >= 1:
                    pe.wait_ge(hid_ft_ready, s)
                for c in range(FC):
                    last = pe.transpose(bank[4][:, tile(c)], hid_sb[s % 2][:, tile(c)], ident[:])
                last.then_inc(hid_turned, 1)

            def project(s):
                pe.wait_ge(hid_ft_ready, s + 1)
                if s >= 1:
                    pe.wait_ge(y_ready, s)
                for c in range(FC):
                    last = pe.matmul(bank[5][:, 0:D], hid_ft[s % 2][:, c, :],
                                     wo_sb[:, bass.ds(expert[s], 1), c, :].rearrange("p e d -> p (e d)"),
                                     start=(c == 0), stop=(c == FC - 1))
                last.then_inc(y_done, 1)

            pe.wait_ge(tile_expert_ready, 1)
            pe.wait_ge(expert_in, 32 * E)
            expert = {}
            turn_slots(0)
            for s in range(SLOT_TILES):
                expert[s] = pe.value_load(tile_expert[0:1, s:s + 1], min_val=0, max_val=E - 1)
                half_hidden(s, 0)
                if s >= 1:
                    turn_hidden(s - 1)
                if s + 1 < SLOT_TILES:
                    turn_slots(s + 1)
                half_hidden(s, 1)
                if s >= 1:
                    project(s - 1)
            turn_hidden(SLOT_TILES - 1)
            project(SLOT_TILES - 1)

        @block.vector
        def _(dve):
            steps = [0]

            def own(ins):
                steps[0] += 1
                ins.then_inc(dve_step, 1)
                dve.wait_ge(dve_step, steps[0])

            def layer_norm(src, nth, dst):
                for t in range(NT):
                    last = dve.bn_stats(stats[:, t, :], src[:, t, :])
                own(last)
                for t in range(NT):
                    last = dve.bn_aggr(mean_var[:, t, :], stats[:, t, :])
                own(last)
                dve.tensor_scalar(var_eps[:], mean_var[:, :, 1], EPS, None, ALU.add).then_inc(var_ready, 1)
                dve.wait_ge(rstd_ready, nth)
                for t in range(NT):
                    last = dve.tensor_scalar(dst[:, t, :], src[:, t, :], mean_var[:, t, 0:1],
                                             rstd[:, t:t + 1], ALU.subtract, ALU.mult)
                last.then_inc(normed, 1)

            dve.wait_ge(x_in, 16)
            layer_norm(x_tok, 1, norm_tok)
            for n in range(2):
                dve.wait_ge(norm_turned, n + 1)
                dve.tensor_copy(norm_ft[:, n * HALF:(n + 1) * HALF], bank[4 + n][:]).then_inc(norm_ft_ready, 1)
            dve.wait_ge(kl_ready, 1)
            halves = [(slice(HF * h, HF * (h + 1)), slice(HF * (1 - h), HF * (2 - h))) for h in range(2)]
            dve.tensor_copy(k_last_split[:, :, :, 1], k_last[:].unsqueeze(1).to_broadcast([128, 2, B]))
            for h, (half, _) in enumerate(halves):
                last = dve.tensor_copy(k_last_split[half, h, :, 0], k_last[half, :])
            own(last)
            for h, (half, other) in enumerate(halves):
                last = dve.tensor_tensor(k_last_split[other, h, :, 0], k_last[half, :],
                                         k_last_split[half, h, :, 0], ALU.subtract)
            last.then_inc(kl_split_ready, 1)
            dve.wait_ge(vec_in, 16)
            for n in range(2):
                for h in range(2):
                    dve.wait_ge(pre_done, 3 + 2 * n + h)
                    last = dve.tensor_scalar(q_twice[:, h, n * HALF:(n + 1) * HALF], bank[2 * n + h][:],
                                             vec_sb[:, (V_BQ0, V_BQ1)[h]], Q_SCALE, ALU.add, ALU.mult)
                last.then_inc(q_ready, 1)

            def split_keys(i, k, first=False):
                p = k % 2
                dve.wait_ge(k_ready, BPT * i + (k + 1))
                if not (first and k < 2):
                    dve.wait_ge(scores_done, G * BPT * i + G * (k - 1))
                for h, (half, _) in enumerate(halves):
                    last = dve.tensor_copy(k_split[p][half, h, 0:KEYS], k_sb[p][half, :])
                last.then_inc(k_high_ready, 1)
                dve.wait_ge(k_high_ready, BPT * i + (k + 1))
                for h, (half, other) in enumerate(halves):
                    last = dve.tensor_tensor(k_split[p][other, h, 0:KEYS], k_sb[p][half, :], k_split[p][half, h, 0:KEYS],
                                             ALU.subtract)
                last.then_inc(k_split_ready, 1)

            def maxima(i, k):
                for g in range(G):
                    dve.wait_ge(scores_done, G * BPT * i + (G * k + g + 1))
                    dve.tensor_reduce(neg_max[k % 2][:, g:g + 1], s_bank[g][:, 0:SKV], AX.X, ALU.max,
                                      negate=True).then_inc(max_ready, 1)

            def turned(i, k, first=False):
                dve.wait_ge(pt_done, 2 * BPT * i + (2 * k + 1))
                if not (first and k < 2):
                    dve.wait_ge(pv_done, BPT * i + (k - 1))
                dve.tensor_copy(pt_sb[k % 2][:, 0, :], pt_bank[0][:]).then_inc(pt0_ready, 1)

            def take_output(i, k):
                dve.wait_ge(pv_done, BPT * i + (k + 1))
                for j in range(J):
                    src = diagonal(o_bank, j)
                    dst = att_tok[SQ * k:SQ * (k + 1), bass.ds(i, 1), :].rearrange(
                        "p t (g j d) -> p (t g) j d", g=G, j=J)[:, :, j, :]
                    last = dve.tensor_copy(dst, src)
                last.then_inc(o_taken, 1)

            def diagonal(tensor, j):
                ap = tensor[SQ * j:SQ * (j + 1), HD * j:HD * (j + 1)].copy()
                (row, p), (one, d) = ap.ap
                return bass.AP(ap.tensor, ap.offset, [[row, p], [128 + J * HD, G], [one, d]])

            def group(i, first=False, last=False):
                for k in range(BPT):
                    if first and k == 0:
                        split_keys(0, 0, True)
                        maxima(0, 0)
                        split_keys(0, 1, True)
                    turned(i, k, first)
                    if not (last and k == BPT - 1):
                        maxima(*((i, k + 1) if k < BPT - 1 else (i + 1, 0)))
                    if k < 2:
                        split_keys(i, k + 2, first)
                    elif not last:
                        split_keys(i + 1, k - 2)
                    take_output(i, k)

            group(0, first=True)
            with dve.Fori(1, B // BPT - 1) as i:
                group(i)
            group(B // BPT - 1, last=True)

            dve.wait_ge(last_kept, B)
            for j in range(J):
                for k in range(BPT):
                    src = sum_last[SQ * j:SQ * (j + 1), :, :, :].rearrange(
                        "p s (t k) g -> p s t k g", k=BPT)[:, :, :, k, :]
                    dst = sum_last_tok[SQ * k:SQ * (k + 1), :, :, :].rearrange(
                        "p s t (g j) -> p s t g j", j=J)[:, :, :, :, j]
                    last = dve.tensor_copy(dst, src)
            own(last)
            heads = [128, NT, H, HD]
            att = att_tok[:].rearrange("p t (h d) -> p t h d", d=HD)
            vl = v_last[:].rearrange("p t (h d) -> p t h d", d=HD)
            dve.wait_ge(v_last_ready, 2)
            own(dve.reciprocal(r_sum[:], sum_last_tok[:, 0, :, :]))
            own(dve.tensor_tensor(vl, vl, sum_last_tok[:, 1, :, :].unsqueeze(3).to_broadcast(heads), ALU.mult))
            own(dve.tensor_tensor(att, att, vl, ALU.add))
            own(dve.tensor_tensor(att, att, r_sum[:].unsqueeze(3).to_broadcast(heads), ALU.mult))
            dve.wait_ge(row_in, 16)
            dve.tensor_tensor(att_tok[:], att_tok[:], row_sb[:, 0, :].unsqueeze(1).to_broadcast([128, NT, D]),
                              ALU.add).then_inc(att_ready, 1)
            dve.wait_ge(xbo_ready, 1)
            dve.wait_ge(wo_done, 1)
            for n in range(2):
                part = x1_tok[:, 4 * n:4 * n + 4, :].rearrange("p t d -> p (t d)")
                last = dve.tensor_tensor(part, bank[n][:], part, ALU.add)
            own(last)
            layer_norm(x1_tok, 2, norm_tok)
            dve.wait_ge(norm_turned, 3)
            dve.tensor_copy(norm_ft[:, 0:HALF], bank[4][:]).then_inc(norm_ft_ready, 1)
            for n in range(2):
                dve.wait_ge(mix_done, 3 + n)
                last = dve.tensor_copy(xb_ft[:, 16 * n:16 * n + 16, 0:SQ - 1],
                                       bank[2 + n][:].rearrange("p (b q) -> p b q", q=SQ)[:, :, 1:SQ])
            own(last)
            dve.wait_ge(xf_ready, 2)
            dve.wait_ge(edges_ready, 2)
            dve.tensor_tensor(s_ft[:].rearrange("p (b q) -> p b q", q=SQ), xf_ft[:], xb_ft[:],
                              ALU.add).then_inc(s_ready, 1)
            dve.wait_ge(gamma_ready, 1)
            dve.wait_ge(mix2_done, 2)
            for n in range(2):
                part = slice(4 * n, 4 * n + 4)
                last = dve.tensor_tensor(x2_tok[:, part, :].rearrange("p t d -> p (t d)"), bank[4 + n][:],
                                         norm_tok[:, part, :].rearrange("p t d -> p (t d)"), ALU.subtract)
            own(last)
            for t in range(NT):
                last = dve.scalar_tensor_tensor(out=x2_tok[:, t, :], in0=x2_tok[:, t, :],
                                                scalar=gamma[:, t:t + 1], in1=norm_tok[:, t, :],
                                                op0=ALU.mult, op1=ALU.add)
            own(last)
            dve.tensor_tensor(x2_tok[:], x2_tok[:], x1_tok[:], ALU.add).then_inc(x2_ready, 1)
            dve.wait_ge(x2_ready, 1)
            layer_norm(x2_tok, 3, rows_tok[:, :, 0, 0:D])
            dve.wait_ge(norm_turned, 5)
            dve.tensor_copy(norm_ft[:, 0:HALF], bank[4][:]).then_inc(norm_ft_ready, 1)
            dve.wait_ge(logits_done, 1)
            own(dve.tensor_copy(logits[:].rearrange("p t e -> p (t e)"), bank[7][:, 0:NT * E]))
            for t in range(NT):
                last = dve.max(top[:, t, :], logits[:, t, :])
            own(last)
            dve.tensor_tensor(top_d[:], top[:, :, 0], top[:, :, 1], ALU.subtract).then_inc(top_ready, 1)
            for t in range(NT):
                last = dve.max_index(top_at[:, t, :], top[:, t, :], logits[:, t, :])
            own(last)
            own(dve.tensor_copy(top_no[:], top_at[:, :, 0:2]))
            dve.wait_ge(consts_ready, 10)
            te = [128, NT, E]
            for c in range(TOPK):
                last = dve.tensor_tensor(pick[:, c, :, :], expert_no[:].unsqueeze(1).to_broadcast(te),
                                         top_no[:, :, c:c + 1].to_broadcast(te), ALU.is_equal)
            own(last)
            dve.tensor_tensor(chosen[:], pick[:, 0, :, :], pick[:, 1, :, :], ALU.add).then_inc(chosen_ready, 1)
            ee = [128, E, E]
            dve.wait_ge(ranks_done, 2)
            own(dve.tensor_tensor(square[:], bank[7][:, 128:128 + E].unsqueeze(2).to_broadcast(ee),
                                  tile_starts[:].unsqueeze(1).to_broadcast(ee), ALU.is_gt))
            own(dve.tensor_reduce(n_tiles[:], square[:], AX.X, ALU.add))
            own(dve.tensor_tensor(square[:], n_tiles[:].unsqueeze(1).to_broadcast(ee), expert_before[:], ALU.mult))
            own(dve.tensor_reduce(first_tile[:], square[:], AX.X, ALU.add))
            own(dve.scalar_tensor_tensor(out=slot[:], in0=first_tile[:].unsqueeze(1).to_broadcast(te),
                                         scalar=128.0, in1=bank[6][:, 0:NT * E].rearrange("p (t e) -> p t e", e=E),
                                         op0=ALU.mult, op1=ALU.add))
            for c in range(TOPK):
                last = dve.tensor_tensor(pick[:, c, :, :], pick[:, c, :, :], slot[:], ALU.mult)
            own(last)
            own(dve.tensor_reduce(slot_of[:], pick[:], AX.X, ALU.add))
            own(dve.tensor_copy(slot_at[:], slot_of[:]))
            dve.tensor_scalar(slot_tile[:], slot_at[:], 7, None, ALU.logical_shift_right)
            own(dve.tensor_scalar(slot_in_tile[:], slot_at[:], 127, None, ALU.bitwise_and))
            ne = [128, TOPK, NT, SLOT_EVEN]
            own(dve.tensor_tensor(in_tile[:], slot_tile[:].unsqueeze(3).to_broadcast(ne),
                                  tile_no[:].unsqueeze(1).unsqueeze(1).to_broadcast(ne), ALU.is_equal))
            dve.tensor_tensor(row_in_tile[:].rearrange("p (c t) s -> p c t s", c=TOPK), in_tile[:],
                              row_back[:].unsqueeze(3).to_broadcast(ne), ALU.mult)
            for c in range(TOPK):
                half = [128, NT, 128]
                dve.tensor_tensor(at_slot[:, NT * c:NT * (c + 1), :], slot_in_tile[:, c, :].unsqueeze(2).to_broadcast(half),
                                  slot_nos[:].unsqueeze(1).to_broadcast(half), ALU.is_equal).then_inc(at_slot_ready, 1)
            se = [1, SLOT_TILES, E]
            own(dve.tensor_tensor(end_tile[:], first_tile[:], n_tiles[:], ALU.add))
            own(dve.tensor_tensor(tile_after[:], tile_no[0:1, 0:SLOT_TILES].unsqueeze(2).to_broadcast(se),
                                  end_tile[0:1, :].unsqueeze(1).to_broadcast(se), ALU.is_ge))
            own(dve.tensor_reduce(tile_expert_f[:], tile_after[:], AX.X, ALU.add))
            dve.tensor_scalar(tile_expert[:], tile_expert_f[:], float(E - 1), None, ALU.min
                              ).then_inc(tile_expert_ready, 1)
            dve.wait_ge(slot_row_done, 1)
            dve.tensor_scalar(slot_row[:], bank[3][:, 0:SLOT_TILES], -1.0, float(TABLE_ROWS), ALU.mult, ALU.add
                              ).then_inc(slot_row_ready, 1)

            def keep_meta(s):
                dve.wait_ge(slot_in[s % SLOT_BUFS], slot_loads(s))
                dve.tensor_copy(slot_meta[:, s, :], slot_sb[s % SLOT_BUFS][:, D:ROW]).then_inc(meta_kept, 1)

            def hidden_features(s):
                dve.wait_ge(hid_turned, s + 1)
                if s >= 2:
                    dve.wait_ge(y_done, s - 1)
                dve.tensor_copy(hid_ft[s % 2][:].rearrange("p c r -> p (c r)"), bank[4][:]).then_inc(hid_ft_ready, 1)

            def weigh_output(s):
                dve.wait_ge(y_done, s + 1)
                dve.wait_ge(meta_kept, s + 1)
                if s >= 2:
                    dve.wait_ge(out_done, 16 * (s - 1))
                dve.tensor_copy(y_tok[s % 2][:], slot_meta[:, s, 1:2])
                dve.tensor_scalar(y_sb[s % 2][:], bank[5][:, 0:D], slot_meta[:, s, 0:1], None,
                                  ALU.mult).then_inc(y_ready, 1)

            keep_meta(0)
            for s in range(SLOT_TILES):
                if s + 1 < SLOT_TILES:
                    keep_meta(s + 1)
                if s >= 1:
                    hidden_features(s - 1)
                dve.wait_ge(silu_ready, s + 1)
                dve.wait_ge(up_half_done, s + 1)
                if s >= 2:
                    dve.wait_ge(hid_turned, s - 1)
                dve.tensor_tensor(hid_sb[s % 2][:], silu_sb[s % 2][:], bank[2 + s % 2][:],
                                  ALU.mult).then_inc(hid_ready, 1)
                if s >= 1:
                    weigh_output(s - 1)
            hidden_features(SLOT_TILES - 1)
            weigh_output(SLOT_TILES - 1)


def kernel(**inputs):
    import numpy as np
    import concourse.bacc as bacc
    from concourse.bass_utils import run_bass_kernel_spmd

    a = {name: np.asarray(value) for name, value in inputs.items()}
    ctx = a["ctx_1024"].transpose(2, 0, 1)
    wq, bq = a["L0_xattn_wq"].T, a["L0_xattn_bq"]
    arrays = {
        "x": a["x"].reshape(TOK, D),
        "ctx_keys": ctx[:, :, 0:KEYS],
        "ctx_last": ctx[:, :, KEYS],
        "weights": np.concatenate([wq[:, 0:HF], wq[:, 0:HF], wq[:, HF:D], wq[:, HF:D], a["L0_xattn_wk"].T, a["L0_xattn_wv"].T,
                                   a["L0_xattn_wo"].T, a["L0_attn_WB"].T, a["L0_attn_WBf"].T], axis=1),
        "vectors": np.stack([np.tile(bq[0:HF], 2), np.tile(bq[HF:D], 2), a["L0_xattn_bk"], a["L0_attn_w1"][0], a["L0_attn_w2"][0],
                             np.broadcast_to(a["L0_attn_b"], (D,))], axis=1),
        "rows": np.stack([a["L0_xattn_bv"], a["L0_xattn_bo"]]),
        "gate": a["L0_ffn_gate_kernel"],
        "w01": np.stack([a["L0_ffn_w0"], a["L0_ffn_w1"]], axis=2),
        "wo": a["L0_ffn_wo"].reshape(E, FC, 128, D).transpose(0, 2, 1, 3),
    }
    arrays = {name: np.ascontiguousarray(value) for name, value in arrays.items()}
    nc = bacc.Bacc("TRN2", target_bir_lowering=False, num_devices=1)
    args = [nc.dram_tensor(name, v.shape, mybir.dt.from_np(v.dtype), kind="ExternalInput").ap()
            for name, v in arrays.items()]
    out = nc.dram_tensor("out", (TOK, D), F32, kind="ExternalOutput").ap()
    build(nc, *args, out)
    result = run_bass_kernel_spmd(nc, [arrays], core_ids=[0])
    return result.results[0]["out"].reshape(B, SQ, D)
```
